# Optimizing a Trainium2 kernel written in Bass

```python
import numpy as np
import jax
import jax.numpy as jnp

def _softmax(x, axis=-1):
    return jax.nn.softmax(x, axis=axis)

def _gelu(x):
    return jax.nn.gelu(x, approximate=True)

def _silu(x):
    return jax.nn.silu(x)

def _sigmoid(x):
    return jax.nn.sigmoid(x)

def _layernorm(x, axis=-1, eps=1e-05):
    m = jnp.mean(x, axis=axis, keepdims=True)
    v = jnp.var(x, axis=axis, keepdims=True)
    return (x - m) / jnp.sqrt(v + eps)

def _scatter_add(tgt, idx, src, axis=0):
    return tgt.at[idx].add(src)

def _segment_sum(src, seg, n):
    return jax.ops.segment_sum(src, seg, n)
kernel_name = 'mk_seq_postln_d1_jaxref_r8_20844c'

def setup_inputs(seed: int=0):
    np.random.seed(seed)
    _w = jnp.asarray

    def _L0_attn_setup():
        import jax, jax.numpy as jnp
        import numpy as np
        HEADS = 16
        SEGS = 8

        def _rotate_half(x):
            x1, x2 = jnp.split(x, 2, axis=-1)
            return jnp.concatenate([-x2, x1], axis=-1)

        def _split_heads(t, h):
            b, n, dim = t.shape
            d = dim // h
            return t.reshape(b, n, h, d).transpose(0, 2, 1, 3).reshape(b * h, n, d)

        def _merge_heads(t, b, h):
            c, n, d = t.shape
            return t.reshape(b, h, n, d).transpose(0, 2, 1, 3).reshape(b, n, h * d)
        key = jax.random.key(seed)
        ks = jax.random.split(key, 5)
        b, n, dim = (2, 512, 128)
        x = jax.random.normal(ks[0], (b, n, dim), dtype=jnp.float32)
        w = lambda k: jax.random.normal(k, (dim, dim), dtype=jnp.float32) * 0.02
        return {'x': x, 'Wq': w(ks[1]), 'Wkv': w(ks[2]), 'Wo': w(ks[3]), 'bo': jnp.zeros((dim,), jnp.float32), 'Wo0': w(ks[4]), 'bo0': jnp.zeros((dim,), jnp.float32)}
    _L0_attn_in = _L0_attn_setup()

    def _L0_ffn_setup():
        import jax, jax.numpy as jnp
        import numpy as np
        B, S, H, F, E = (4, 256, 128, 512, 8)
        key = jax.random.key(seed)
        ks = jax.random.split(key, 8)
        s = 1.0 / np.sqrt(H)
        sf = 1.0 / np.sqrt(F)
        return {'x': jax.random.normal(ks[0], (B, S, H), jnp.float32), 'wr': jax.random.uniform(ks[1], (H, E), jnp.float32, -s, s), 'br': jax.random.uniform(ks[2], (E,), jnp.float32, -s, s), 'w1': jax.random.uniform(ks[3], (E, H, F), jnp.float32, -s, s), 'b1': jax.random.uniform(ks[4], (E, F), jnp.float32, -s, s), 'w2': jax.random.uniform(ks[5], (E, F, H), jnp.float32, -sf, sf), 'b2': jax.random.uniform(ks[6], (E, H), jnp.float32, -sf, sf)}
    _L0_ffn_in = _L0_ffn_setup()
    _d = {'L0_attn_x': _L0_attn_in['x'], 'L0_attn_Wq': _L0_attn_in['Wq'], 'L0_attn_Wkv': _L0_attn_in['Wkv'], 'L0_attn_Wo': _L0_attn_in['Wo'], 'L0_attn_bo': _L0_attn_in['bo'], 'L0_attn_Wo0': _L0_attn_in['Wo0'], 'L0_attn_bo0': _L0_attn_in['bo0'], 'L0_ffn_wr': _L0_ffn_in['wr'], 'L0_ffn_br': _L0_ffn_in['br'], 'L0_ffn_w1': _L0_ffn_in['w1'], 'L0_ffn_b1': _L0_ffn_in['b1'], 'L0_ffn_w2': _L0_ffn_in['w2'], 'L0_ffn_b2': _L0_ffn_in['b2']}
    _x0 = _d['L0_attn_x']
    _d['L0_attn_x'] = jax.random.normal(jax.random.fold_in(jax.random.key(seed), 1), (32, 256, 128), dtype=_x0.dtype)
    del _x0
    return _d

def reference(L0_attn_x, L0_attn_Wq, L0_attn_Wkv, L0_attn_Wo, L0_attn_bo, L0_attn_Wo0, L0_attn_bo0, L0_ffn_wr, L0_ffn_br, L0_ffn_w1, L0_ffn_b1, L0_ffn_w2, L0_ffn_b2):

    def _L0_attn_ref(x, Wq, Wkv, Wo, bo, Wo0, bo0):
        import jax, jax.numpy as jnp
        import numpy as np
        HEADS = 16
        SEGS = 8

        def _rotate_half(x):
            x1, x2 = jnp.split(x, 2, axis=-1)
            return jnp.concatenate([-x2, x1], axis=-1)

        def _split_heads(t, h):
            b, n, dim = t.shape
            d = dim // h
            return t.reshape(b, n, h, d).transpose(0, 2, 1, 3).reshape(b * h, n, d)

        def _merge_heads(t, b, h):
            c, n, d = t.shape
            return t.reshape(b, h, n, d).transpose(0, 2, 1, 3).reshape(b, n, h * d)
        b, n, dim = x.shape
        h = HEADS
        d = dim // h
        s = SEGS
        m = n // s
        mask_value = -jnp.finfo(x.dtype).max
        q = _split_heads(x @ Wq, h)
        kv = _split_heads(x @ Wkv, h)
        inv_freq = 1.0 / 10000.0 ** (jnp.arange(0, d, 2, dtype=jnp.float32) / d)
        freqs = jnp.arange(n, dtype=jnp.float32)[:, None] * inv_freq[None, :]
        rot = jnp.concatenate([freqs, freqs], axis=-1)[None]
        cos, sin = (jnp.cos(rot), jnp.sin(rot))
        q = q * cos + _rotate_half(q) * sin
        kv = kv * cos + _rotate_half(kv) * sin
        q = q * d ** (-0.5)
        qs = q.reshape(-1, s, m, d)
        kvs = kv.reshape(-1, s, m, d)
        kvs_ccs = jnp.concatenate([kvs[:, :-1], kvs[:, 1:]], axis=2)
        qs_ccs = qs[:, 1:]
        lsim = jnp.einsum('csmd,csnd->csmn', qs_ccs, kvs_ccs)
        causal = jnp.triu(jnp.ones((m, m), dtype=bool), 1)
        lsim = jnp.concatenate([lsim[..., :m], jnp.where(causal, mask_value, lsim[..., m:])], axis=-1)
        attn0 = jnp.einsum('csmd,csnd->csmn', qs[:, :1], kvs[:, :1])
        attn0 = jnp.where(causal, mask_value, attn0)
        attn0 = jax.nn.softmax(attn0, axis=-1)
        attn1 = jax.nn.softmax(lsim, axis=-1)
        out0 = jnp.einsum('csij,csjd->csid', attn0, kvs[:, :1]).reshape(-1, m, d)
        out1 = jnp.einsum('csij,csjd->csid', attn1, kvs_ccs).reshape(-1, (s - 1) * m, d)
        out0 = _merge_heads(out0, b, h) @ Wo0 + bo0
        out1 = _merge_heads(out1, b, h) @ Wo + bo
        return jnp.concatenate([out0, out1], axis=1)

    def _L0_ffn_ref(x, wr, br, w1, b1, w2, b2):
        import jax, jax.numpy as jnp
        import numpy as np
        B, S, H, F, E = (4, 256, 128, 512, 8)
        scores = jnp.einsum('bsh,he->bse', x, wr) + br
        expert_id = jnp.argmax(scores, axis=-1)
        h = jnp.einsum('bsh,ehf->ebsf', x, w1) + b1[:, None, None, :]
        h = jax.nn.gelu(h, approximate=False)
        y = jnp.einsum('ebsf,efh->ebsh', h, w2) + b2[:, None, None, :]
        one_hot = jax.nn.one_hot(expert_id, E, dtype=x.dtype)
        out = jnp.einsum('ebsh,bse->bsh', y, one_hot)
        return out
    x = L0_attn_x
    x = _layernorm(x + _L0_attn_ref(x, L0_attn_Wq, L0_attn_Wkv, L0_attn_Wo, L0_attn_bo, L0_attn_Wo0, L0_attn_bo0), axis=-1)
    x = _layernorm(x + _L0_ffn_ref(x, L0_ffn_wr, L0_ffn_br, L0_ffn_w1, L0_ffn_b1, L0_ffn_w2, L0_ffn_b2), axis=-1)
    return x

_drawn_inputs = setup_inputs


def setup_inputs(seed=0):
    import zlib

    import numpy as np

    out = dict(_drawn_inputs(seed))
    spreads = {'L0_attn_bo': (0.0, 0.1), 'L0_attn_bo0': (0.0, 0.1)}
    factors = {'L0_attn_Wq': 8.0,
     'L0_attn_Wkv': 2.697,
     'L0_attn_Wo': 2.929,
     'L0_attn_Wo0': 5.347,
     'L0_ffn_b1': 3.136}
    for name, (base, spread) in spreads.items():
        noise = np.random.default_rng([zlib.crc32(name.encode()), seed]).standard_normal(out[name].shape)
        drawn = base * np.exp(spread * noise) if base else spread * noise
        out[name] = jnp.asarray(drawn.astype(out[name].dtype))
    for name, factor in factors.items():
        out[name] = (out[name] * factor).astype(out[name].dtype)
    return out
```

```python
from contextlib import ExitStack

import numpy as np

import concourse.bass as bass
from concourse import mybir

F32 = mybir.dt.float32
BF16 = mybir.dt.bfloat16
I32 = mybir.dt.int32
ACT = mybir.ActivationFunctionType
ALU = mybir.AluOpType
AX = mybir.AxisListType

P = 128
BATCHES, SEQ, DIM = 32, 256, 128
HEADS, HD = 16, 8
SEG = 32
WIN = 2 * SEG
UNITS = BATCHES * SEQ // P
TOKENS = BATCHES * SEQ
EXPERTS, FF = 8, 512
CH = FF // P
ROW = DIM + 4
REGION = TOKENS + P
TILES = 72
RING = 8
MASKED = -1e30
EPS = 1e-5
SCALE = float(HD) ** -0.5

CF = {}
CB = {}


def _layout(table, widths):
    at = 0
    for name, w in widths:
        table[name] = (at, at + w)
        at += w
    return at


NF = _layout(CF, [("ident", P), ("cos", SEQ), ("sin", SEQ), ("own8", 8), ("own4", 4), ("pairs", WIN), ("tok", 4),
                  ("rev", 8), ("first", 8), ("part", 1), ("half", 1), ("upto", 64), ("before", 64), ("tile", TILES)])
NB = _layout(CB, [("ident", P), ("mask", 2 * 512), ("pick", 2 * 512), ("below", P), ("ones", P)])


def constants():
    f = np.zeros((P, NF), np.float32)
    b = np.zeros((P, NB), np.float32)

    def put(a, table, name, v):
        lo, hi = table[name]
        a[:, lo:hi] = np.broadcast_to(v, (P, hi - lo))

    p = np.arange(P)
    put(f, CF, "ident", np.eye(P))
    inv_freq = (np.float32(1.0) / np.float32(10000.0) ** (np.arange(0, HD, 2, dtype=np.float32) / np.float32(HD)))
    angle = np.arange(SEQ, dtype=np.float32)[:, None] * inv_freq.astype(np.float32)[None, :]
    angle = np.concatenate([angle, angle], axis=-1).astype(np.float32)
    d = p % HD
    put(f, CF, "cos", np.cos(angle)[:, d].T)
    put(f, CF, "sin", (np.sin(angle)[:, d] * np.where(d < HD // 2, -1.0, 1.0)[None, :]).T)
    put(f, CF, "own8", (p[:, None] // HD % 8 == np.arange(8)[None]))
    put(f, CF, "own4", (p[:, None] // HD % 4 == np.arange(4)[None]))
    c = np.arange(WIN)
    put(f, CF, "pairs", (p[:, None] // 64 == c[None] // 32) & (p[:, None] % 32 == c[None] % 32))
    put(f, CF, "tok", p[:, None] + P * np.arange(4)[None])
    put(f, CF, "rev", 8.0 - np.arange(8)[None])
    put(f, CF, "first", REGION * np.arange(8)[None])
    put(f, CF, "part", p[:, None])
    put(f, CF, "half", -0.5)
    put(f, CF, "upto", 128.0 * np.arange(64)[None])
    e = np.arange(8)
    put(f, CF, "before", (e[None, :] <= e[:, None]).reshape(1, 64))
    put(f, CF, "tile", np.arange(TILES)[None])
    put(b, CB, "ident", np.eye(P))
    mask = np.zeros((P, 2, 2, 8, SEG), np.float32)
    block, query = p // SEG % 2, p % SEG
    key = np.arange(SEG)
    causal = (block[:, None] == 1) & (key[None, :] > query[:, None])
    mask += np.where(causal, MASKED, 0.0)[:, None, None, None, :]
    mask[:SEG, 0, 0] = MASKED
    put(b, CB, "mask", mask.reshape(P, -1))
    pick = np.zeros((4, 32, 2, 2, 8, SEG), np.float32)
    for half in range(2):
        for pair in range(2):
            for h in range(8):
                pick[:3, half * 16 + pair * 8 + h, half, pair, h] = 1.0
    put(b, CB, "pick", pick.reshape(P, -1))
    put(b, CB, "below", p[:, None] < p[None, :])
    put(b, CB, "ones", 1.0)
    return f, b.astype(mybir.dt.np(BF16))


def layer(nc, x, wq, wkv, wo, bo, wo0, bo0, wr, br, w1, b1, w2, b2, cf, cb, out):
    ctx = ExitStack()
    with ctx:
        def sb(name, shape, dt=F32):
            return ctx.enter_context(nc.sbuf_tensor(name, shape, dt))

        def psum(name, shape):
            return ctx.enter_context(nc.psum_tensor(name, shape, F32))

        def sem(name):
            return ctx.enter_context(nc.semaphore(name))

        routed = nc.dram_tensor("routed_rows", [EXPERTS * REGION + P, ROW], F32).ap()
        x_rows = x.rearrange("b (c p) d -> b p c d", p=P)
        out_rows = out.rearrange("b n d -> (b n) d")

        cf_sb, cb_sb = sb("cf_sb", [P, NF]), sb("cb_sb", [P, NB], BF16)
        wq_sb, wkv_sb, wo_sb, wo0_sb = (sb(n, [P, P]) for n in ("wq_sb", "wkv_sb", "wo_sb", "wo0_sb"))
        wo_own, wo0_own = sb("wo_own", [P, 4, P]), sb("wo0_own", [P, 4, P])
        wq_rot, wkv_rot = sb("wq_rot", [P, P]), sb("wkv_rot", [P, P])
        wr_sb, br_sb = sb("wr_sb", [P, 8]), sb("br_sb", [P, 8])
        bo_sb = sb("bo_sb", [P, 2, P])
        w1_sb = sb("w1_sb", [P, EXPERTS * FF])
        w2_sb = sb("w2_sb", [P, EXPERTS * CH * P])
        bias_in = sb("bias_in", [EXPERTS, FF + P])
        bias_rest = sb("bias_rest", [EXPERTS, 2, FF + P])
        bias_part = sb("bias_part", [EXPERTS, 3, FF + P], BF16)
        bias3 = sb("bias3", [3, EXPERTS, FF + P], BF16)

        def cfs(name, rows=P):
            lo, hi = CF[name]
            return cf_sb[0:rows, lo:hi]

        def cbs(name, rows=P):
            lo, hi = CB[name]
            return cb_sb[0:rows, lo:hi]

        ident, ident_b = cfs("ident"), cbs("ident")
        mask = cbs("mask").rearrange("p (c n) -> p c n", c=2)
        pick = cbs("pick", 96).rearrange("p (c n) -> p c n", c=2)

        x_in = sb("x_in", [P, 2, 2, P])
        x_bias = sb("x_bias", [P, 4, P])
        xT = sb("xT", [P, 2, SEQ])
        k_cos, k_sin, q_cos, q_sin = (sb(n, [P, SEQ]) for n in ("k_cos", "k_sin", "q_cos", "q_sin"))
        qT = sb("qT", [P, 2, SEQ])
        kv_win = sb("kv_win", [P, 2, 8, 2, SEG])
        k_own = sb("k_own", [P, 2, 8, SEQ])
        v_win = sb("v_win", [P, 2, 4, P])
        row_max = sb("row_max", [P, 2, 32])
        neg_max, rest1, rest2 = sb("neg_max", [32, 64]), sb("rest1", [32, 64]), sb("rest2", [32, 64])
        part2 = sb("part2", [32, 64], BF16)
        max_part = sb("max_part", [96, 2, P], BF16)
        prob = sb("prob", [P, 2, 1024])
        prob_t = sb("prob_t", [P, 2, 1024])
        tree = sb("tree", [P, 32, 16])
        tree2 = sb("tree2", [P, 32, 8])
        tree3 = sb("tree3", [P, 32, 4])
        tree4 = sb("tree4", [P, 32, 2])
        key_sum = sb("key_sum", [P, 32])
        sum_wide = sb("sum_wide", [P, 2, P])
        total_sb = sb("total_sb", [P, P])
        headed = sb("headed", [P, 2, 4, P])
        resid = sb("resid", [P, 2, P])
        stats, mean_var, veps, rstd = sb("stats", [P, 6]), sb("mean_var", [P, 2, 2]), sb("veps", [P, 1]), sb("rstd", [P, 1])
        row = sb("row", [P, 4, ROW])
        x1T = sb("x1T", [P, 2, P])
        score, top, keyed, ktop = sb("score", [P, 8]), sb("top", [P, 1]), sb("keyed", [P, 8]), sb("ktop", [P, 1])
        chosen = sb("chosen", [P, 2, 8], BF16)
        base = sb("base", [P, 2, 8])
        place8, place_prod, place = sb("place8", [P, 8]), sb("place_prod", [P, 8]), sb("place", [P, 1])
        place_i = sb("place_i", [P, 4], I32)

        pad = sb("pad", [P, ROW])
        pad_at, pad_i = sb("pad_at", [P, 8]), sb("pad_i", [P, 8], I32)
        count8 = sb("count8", [1, 8])
        over, tiles8 = sb("over", [1, 8, 64]), sb("tiles8", [1, 8])
        cum_prod, cum8, jump8 = sb("cum_prod", [1, 8, 8]), sb("cum8", [1, 8]), sb("jump8", [1, 8])
        past, past_jump = sb("past", [1, TILES, 8]), sb("past_jump", [1, TILES, 8])
        tile_e, tile_j, tile_row = sb("tile_e", [1, TILES]), sb("tile_j", [1, TILES]), sb("tile_row", [1, TILES])
        tile_e_i, tile_row_i = sb("tile_e_i", [1, TILES], I32), sb("tile_row_i", [1, TILES], I32)

        rows_in = sb("rows_in", [P, RING, ROW])
        rowsT = sb("rowsT", [P, 2, P])
        hid = sb("hid", [P, 2, FF])
        hidT = sb("hidT", [P, 2, FF])
        sum2 = sb("sum2", [P, 2, P])
        stats2, mv2 = sb("stats2", [P, 6]), sb("mv2", [P, 2, 2])
        veps2, rstd2 = sb("veps2", [P, 1]), sb("rstd2", [P, 2, 1])
        done_rows = sb("done_rows", [P, RING, P])
        token_i = sb("token_i", [P, RING], I32)

        S = psum("S", [P, 4, 512])
        O = psum("O", [P, 2, 512])
        B6 = psum("B6", [P, 512])
        B7 = psum("B7", [P, 512])

        weights_in, experts_in, biases_in, bias_parts_in = sem("weights_in"), sem("experts_in"), sem("biases_in"), sem("bias_parts_in")
        x_loaded = [sem(f"x_loaded{i}") for i in range(2)]
        setup_dve, setup_pool = sem("setup_dve"), sem("setup_pool")
        xT_made, xT_ready = sem("xT_made"), sem("xT_ready")
        k_made, k_turned, k_ready, k_own_ready = sem("k_made"), sem("k_turned"), sem("k_ready"), sem("k_own_ready")
        q_made, q_turned, q_ready = sem("q_made"), sem("q_turned"), sem("q_ready")
        v_made, v_ready = sem("v_made"), sem("v_ready")
        x_bias_ready = sem("x_bias_ready")
        scores_made, max_ready, max_turned = sem("scores_made"), sem("max_ready"), sem("max_turned")
        neg_ready, part1_ready, rest1_ready, part2_ready, rest2_ready, max_parts_ready = (
            sem(n) for n in ("neg_ready", "part1_ready", "rest1_ready", "part2_ready", "rest2_ready", "max_parts_ready"))
        shifted, prob_ready, prob_t_ready = sem("shifted"), sem("prob_ready"), sem("prob_t_ready")
        tree_step, key_sum_ready, sum_wide_ready, total_made, total_ready = (
            sem(n) for n in ("tree_step", "key_sum_ready", "sum_wide_ready", "total_made", "total_ready"))
        values_made, headed_ready = sem("values_made"), sem("headed_ready")
        attn_made, resid_ready, stats_ready, mv_ready, veps_ready, rstd_ready = (
            sem(n) for n in ("attn_made", "resid_ready", "stats_ready", "mv_ready", "veps_ready", "rstd_ready"))
        row_ready, x1T_made, x1T_ready, route_made = sem("row_ready"), sem("x1T_made"), sem("x1T_ready"), sem("route_made")
        score_ready, top_ready, keyed_ready, ktop_ready, chosen_ready = (
            sem(n) for n in ("score_ready", "top_ready", "keyed_ready", "ktop_ready", "chosen_ready"))
        rank_made, place8_ready, place_ready, place_i_ready, base_ready = (
            sem(n) for n in ("rank_made", "place8_ready", "place_ready", "place_i_ready", "base_ready"))
        token_set = sem("token_set")
        row_out = [sem(f"row_out{i}") for i in range(4)]
        table_step, table_ready, pad_at_ready, pads_out = sem("table_step"), sem("table_ready"), sem("pad_at_ready"), sem("pads_out")
        rows_loaded = [sem(f"rows_loaded{i}") for i in range(RING)]
        rowsT_made, rowsT_ready, hid_made, hid_ready, hidT_made, hidT_ready, y_made = (
            sem(n) for n in ("rowsT_made", "rowsT_ready", "hid_made", "hid_ready", "hidT_made", "hidT_ready", "y_made"))
        sum2_ready, stats2_ready, mv2_ready, veps2_ready, rstd2_ready, done_ready, token_ready = (
            sem(n) for n in ("sum2_ready", "stats2_ready", "mv2_ready", "veps2_ready", "rstd2_ready", "done_ready", "token_ready"))
        tile_out = [sem(f"tile_out{i}") for i in range(RING)]

        WEIGHTS = 16 * 11

        def held(eng, count):
            return count if isinstance(count, int) else eng.compute_val(count)

        def settled(eng):
            eng.wait_ge(setup_pool, 1)

        def unit_loop(eng, slot):
            for k in range(8):
                slot(k, k // 4 * 2, k, k, k % 4)
            with eng.Fori(2, UNITS // 4 - 1) as r:
                k0, b0 = eng.snap(r * 4), eng.snap(r * 2)
                for j in range(4):
                    slot(k0 + j, b0, 8, UNITS - 5, j)
            for j in range(4):
                k = UNITS - 4 + j
                slot(k, UNITS // 2 - 2, k, k, j)

        def tile_loop(eng, slot):
            for t in range(2 * RING):
                slot(t, t // RING, t, t, t % RING)
            with eng.Fori(2, TILES // RING - 1) as r:
                t0 = eng.snap(r * RING)
                for j in range(RING):
                    slot(t0 + j, r, 2 * RING, TILES - RING - 1, j)
            for j in range(RING):
                t = TILES - RING + j
                slot(t, TILES // RING - 1, t, t, j)

        block = ctx.enter_context(nc.Block())

        @block.sync
        def _(sp):
            sp.dma_start(cf_sb[:, :], cf).then_inc(weights_in, 16)
            sp.dma_start(x_in[:, 0], x_rows[0]).then_inc(x_loaded[0], 16)
            sp.dma_start(wq_sb[:, :], wq).then_inc(weights_in, 16)
            sp.dma_start(wkv_sb[:, :], wkv).then_inc(weights_in, 16)
            sp.dma_start(x_in[:, 1], x_rows[1]).then_inc(x_loaded[1], 16)
            sp.dma_start(cb_sb[:, :], cb).then_inc(weights_in, 16)
            sp.dma_start(wo_sb[:, :], wo).then_inc(weights_in, 16)
            sp.dma_start(wo0_sb[:, :], wo0).then_inc(weights_in, 16)
            sp.dma_start(wr_sb[:, :], wr).then_inc(weights_in, 16)
            sp.dma_start(br_sb[:, :], br.partition_broadcast(P)).then_inc(weights_in, 16)
            sp.dma_start(bo_sb[:, 1], bo.partition_broadcast(P)).then_inc(weights_in, 16)
            sp.dma_start(bo_sb[SEG:P, 0], bo.partition_broadcast(P - SEG)).then_inc(weights_in, 16)
            sp.dma_start(bo_sb[0:SEG, 0], bo0.partition_broadcast(SEG)).then_inc(weights_in, 16)
            sp.dma_start(bias_in[:, 0:FF], b1).then_inc(biases_in, 16)
            sp.dma_start(bias_in[:, FF:], b2).then_inc(biases_in, 16)
            sp.dma_start(w1_sb[:, :].rearrange("p (e f) -> p e f", e=EXPERTS), w1.rearrange("e h f -> h e f")).then_inc(experts_in, 16)
            sp.dma_start(w2_sb[:, :].rearrange("p (e c n) -> p e c n", e=EXPERTS, c=CH),
                         w2.rearrange("e (c p) n -> p e c n", p=P)).then_inc(experts_in, 16)
            sp.wait_ge(setup_dve, 9)
            for part in range(3):
                sp.dma_start(bias3[part:part + 1].rearrange("a e n -> a (e n)"),
                             bias_part[:, part, :]).then_inc(bias_parts_in, 16)

            def load(batch, par):
                sp.wait_ge(x_bias_ready, batch - 1)
                sp.wait_ge(xT_made, batch - 1)
                sp.dma_start(x_in[:, par], x_rows[bass.ds(batch, 1)].rearrange("b p c d -> (b p) c d")
                             if not isinstance(batch, int) else x_rows[batch]).then_inc(x_loaded[par], 16)

            with sp.Fori(1, BATCHES // 2) as r:
                b0 = sp.snap(r * 2)
                load(b0, 0)
                load(b0 + 1, 1)

            sp.wait_ge(table_ready, 1)
            for i in range(4):
                sp.wait_ge(row_out[i], 16 * (UNITS // 4))
            sp.wait_ge(pads_out, 16 * (EXPERTS + 1))

            def slot(t, r, lo, hi, j):
                if lo >= RING:
                    sp.wait_ge(sum2_ready, t - (RING - 1))
                    sp.wait_ge(token_ready, t - (RING - 1))
                at = sp.value_load(tile_row_i[0:1, bass.ds(t, 1)], min_val=0, max_val=EXPERTS * REGION)
                sp.dma_start(rows_in[:, j], routed[bass.ds(at, P), :]).then_inc(rows_loaded[j], 16)

            tile_loop(sp, slot)
            for i in range(RING):
                sp.wait_ge(tile_out[i], 16 * (TILES // RING))

        @block.tensor
        def _(pe):
            def turn_x(batch, par):
                pe.wait_ge(x_loaded[par], (batch // 2 + 1) * 16 if isinstance(batch, int) else batch * 8 + (8 if par else 16))
                for c in range(2):
                    mm = pe.transpose(B6[:, c * P:(c + 1) * P], x_in[:, par, c], ident)
                mm.then_inc(xT_made, 1)

            def project(batch, par, w, w_rot, made):
                pe.wait_ge(xT_ready, batch + 1)
                pe.matmul(B6[:, 0:SEQ], w[:, :], xT[:, par], start=True, stop=True)
                pe.matmul(B6[:, SEQ:], w_rot[:, :], xT[:, par], start=True, stop=True).then_inc(made, 1)

            def turn_v(batch, par):
                pe.wait_ge(k_ready, batch + 1)
                pe.wait_ge(q_turned, batch + 1)
                for pair in range(4):
                    mm = pe.transpose(B6[:, pair * P:(pair + 1) * P],
                                      kv_win[:, par, 2 * pair:2 * pair + 2].rearrange("p s b k -> p (s b k)"), ident)
                mm.then_inc(v_made, 1)

            def scores(c, par):
                for half in range(2):
                    pe.matmul(S[:, 2 * c + half], ident_b, mask[:, c], start=True, stop=False, skip_group_check=True)
                for pair in range(2):
                    for half in range(2):
                        rows = slice(64 * half, 64 * half + 64)
                        for s2 in range(2):
                            for blk in range(2):
                                s = 4 * c + 2 * pair + s2
                                if s - 1 + blk < 0:
                                    continue
                                quad = 32 * (2 * s2 + blk)
                                mm = pe.matmul(S[quad:quad + 32, 2 * c + half, 256 * pair:256 * pair + 256],
                                               qT[rows, par, SEG * s:SEG * s + SEG],
                                               k_own[rows, par, :, SEG * (s - 1 + blk):SEG * (s + blk)],
                                               start=False, stop=False, skip_group_check=True)
                mm.then_inc(scores_made, 1)

            def shift(c, ring):
                for half in range(2):
                    mm = pe.matmul(S[:, 2 * c + half], max_part[:, ring], pick[:, half], start=False, stop=True,
                                   skip_group_check=True)
                mm.then_inc(shifted, 1)

            def slot(k, b, lo, hi, j):
                c, par = j % 2, j // 2
                nb = b + (j + 3) // 2 if j % 2 else b + j // 2 + 1
                npar = ((j + 3) // 2 if j % 2 else j // 2 + 1) % 2
                prep = (hi + (3 if j % 2 else 2)) // 2 < BATCHES
                pe.wait_ge(max_ready, k + 1)
                if lo >= 1:
                    if (hi + 2) // 2 < BATCHES and j % 2 == 0:
                        pe.wait_ge(k_turned, nb + 1)
                    elif (hi + 1) // 2 < BATCHES and j % 2:
                        pe.wait_ge(v_ready, nb)
                    else:
                        pe.wait_ge(x1T_ready, k - 2)
                pe.transpose(B6[0:32, 0:P], row_max[:, c], ident).then_inc(max_turned, 1)
                if lo >= 1:
                    if lo >= 3:
                        pe.wait_ge(base_ready, k - 2)
                    totals(k - 1)
                if hi + 1 < UNITS:
                    if lo >= 1:
                        pe.wait_ge(prob_ready, k)
                    if j % 2 == 1:
                        pe.wait_ge(q_ready, b + (j + 1) // 2 + 1)
                        pe.wait_ge(k_own_ready, b + (j + 1) // 2 + 1)
                    scores((c + 1) % 2, (j + 1) // 2 % 2)
                pe.wait_ge(max_parts_ready, k + 1)
                shift(c, c)
                if lo >= 2:
                    pe.wait_ge(row_ready, k - 1)
                    pe.transpose(B6[:, 0:P], row[:, (j - 2) % 4, 0:P], ident).then_inc(x1T_made, 1)
                if lo >= 1:
                    output(k - 1, (c + 1) % 2)
                if prep:
                    if lo >= 2:
                        pe.wait_ge(x1T_ready, k - 1)
                    if j % 2:
                        turn_x(nb, npar)
                    else:
                        project(nb, npar, wq_sb, wq_rot, q_made)
                if lo >= 2:
                    pe.wait_ge(x1T_ready, k - 1)
                    pe.wait_ge(resid_ready, k)
                    pe.matmul(B7[:, 0:8], x1T[:, c], wr_sb[:, :], start=True, stop=True).then_inc(route_made, 1)
                if prep:
                    if j % 2:
                        project(nb, npar, wkv_sb, wkv_rot, k_made)
                    else:
                        turn_v(nb, npar)
                values(k, b, lo, j)
                if lo >= 2:
                    rank(k - 2, c)

            def totals(u):
                pe.wait_ge(sum_wide_ready, u + 1)
                for pair in range(2):
                    mm = pe.matmul(B7[:, 64 * pair:64 * pair + 64], sum_wide[:, pair], cfs("pairs"), start=True, stop=True)
                mm.then_inc(total_made, 1)

            def values(k, b, lo, j):
                c, par = j % 2, j // 2
                probs, batches = held(pe, k + 1), held(pe, b + j // 2 + 1)
                settled(pe)
                pe.wait_ge(prob_t_ready, probs)
                if lo >= 1:
                    pe.wait_ge(headed_ready, k)
                if j % 2 == 0:
                    pe.wait_ge(v_ready, batches)
                for pair in range(2):
                    for s2 in range(2):
                        rows = slice(64 * s2, 64 * s2 + 64)
                        for g in range(4):
                            at = 512 * (g // 2) + 256 * pair + 128 * (g % 2)
                            mm = pe.matmul(O[32 * g:32 * g + 32, s2, 128 * pair:128 * pair + 128],
                                           v_win[rows, par, 2 * c + pair, 32 * g:32 * g + 32],
                                           prob_t[rows, c, at:at + 128], start=True, stop=True)
                mm.then_inc(values_made, 1)

            def output(u, c):
                pe.wait_ge(headed_ready, u + 1)
                for h in range(4):
                    mm = pe.matmul(B7[:, 0:P], headed[:, c, h], wo_own[:, h], start=(h == 0), stop=(h == 3))
                if c == 0:
                    for h in range(4):
                        mm = pe.matmul(B7[0:SEG, 0:P], headed[:, c, h, 0:SEG], wo0_own[:, h], start=(h == 0), stop=(h == 3))
                mm.then_inc(attn_made, 1)

            def rank(u, c):
                pe.wait_ge(chosen_ready, u + 1)
                pe.matmul(B7[:, 0:8], cbs("below"), chosen[:, c], start=True, stop=True)
                pe.matmul(B7[:, 8:16], cbs("ones"), chosen[:, c], start=True, stop=True).then_inc(rank_made, 1)

            pe.wait_ge(weights_in, WEIGHTS)
            pe.wait_ge(setup_dve, 3)
            turn_x(0, 0)
            project(0, 0, wkv_sb, wkv_rot, k_made)
            pe.wait_ge(k_turned, 1)
            project(0, 0, wq_sb, wq_rot, q_made)
            turn_v(0, 0)
            pe.wait_ge(v_ready, 1)
            turn_x(1, 1)
            project(1, 1, wkv_sb, wkv_rot, k_made)
            pe.wait_ge(k_own_ready, 1)
            pe.wait_ge(q_ready, 1)
            scores(0, 0)
            pe.wait_ge(k_turned, 2)
            unit_loop(pe, slot)

            last = UNITS - 1

            def turn_and_route(u, c):
                pe.wait_ge(row_ready, u + 1)
                pe.transpose(B6[:, 0:P], row[:, u % 4, 0:P], ident).then_inc(x1T_made, 1)
                pe.wait_ge(x1T_ready, u + 1)
                pe.matmul(B7[:, 0:8], x1T[:, c], wr_sb[:, :], start=True, stop=True).then_inc(route_made, 1)
                rank(u, c)

            pe.wait_ge(base_ready, last - 1)
            totals(last)
            output(last, 1)
            pe.wait_ge(resid_ready, UNITS)
            turn_and_route(last - 1, 0)
            pe.wait_ge(base_ready, last)
            turn_and_route(last, 1)

            ones3 = cbs("ones", 3)

            def turn_rows(t, r, tlo, j):
                pe.wait_ge(rows_loaded[j], r * 16 + 16)
                if tlo >= 2:
                    pe.wait_ge(rowsT_ready, t)
                pe.transpose(B6[:, 0:P], rows_in[:, j, 0:P], ident).then_inc(rowsT_made, 1)

            def first_product(t, tlo, j):
                e = pe.value_load(tile_e_i[0:1, bass.ds(t, 1)], min_val=0, max_val=EXPERTS - 1)
                pe.wait_ge(rowsT_ready, t + 1)
                if tlo >= 2:
                    pe.wait_ge(hid_ready, t - 1)
                pe.matmul(S[:, j % 2], ones3, b13[:, bass.ds(e * (FF + P), FF)], start=True, stop=False)
                pe.matmul(S[:, j % 2], rowsT[:, j % 2], w1_sb[:, bass.ds(e * FF, FF)], start=False, stop=True).then_inc(hid_made, 1)

            def turn_hidden(t, tlo, j):
                pe.wait_ge(hid_ready, t + 1)
                if tlo >= 2:
                    pe.wait_ge(hidT_ready, t - 1)
                for c in range(CH):
                    mm = pe.transpose(S[:, 2 + j % 2, c * P:(c + 1) * P], hid[:, j % 2, c * P:(c + 1) * P], ident)
                mm.then_inc(hidT_made, 1)

            def second_product(t, tlo, j):
                e = pe.value_load(tile_e_i[0:1, bass.ds(t, 1)], min_val=0, max_val=EXPERTS - 1)
                pe.wait_ge(hidT_ready, t + 1)
                if tlo >= 2:
                    pe.wait_ge(sum2_ready, t - 1)
                pe.matmul(O[:, j % 2, 0:P], ones3, b13[:, bass.ds(e * (FF + P) + FF, P)], start=True, stop=False)
                for c in range(CH):
                    mm = pe.matmul(O[:, j % 2, 0:P], hidT[:, j % 2, c * P:(c + 1) * P],
                                   w2_sb[:, bass.ds(e * (CH * P) + c * P, P)], start=False, stop=(c == CH - 1))
                mm.then_inc(y_made, 1)

            b13 = bias3[:, :, :].rearrange("a e n -> a (e n)")
            pe.wait_ge(table_ready, 1)
            pe.wait_ge(bias_parts_in, 48)
            pe.wait_ge(experts_in, 32)
            turn_rows(0, 0, 0, 0)
            pe.wait_ge(rowsT_ready, 1)
            turn_rows(1, 0, 1, 1)
            first_product(0, 0, 0)

            def tile_slot(t, r, lo, hi, j):
                if hi + 2 < TILES:
                    turn_rows(t + 2, r + (j + 2) // RING, lo + 2, (j + 2) % RING)
                if hi + 1 < TILES:
                    first_product(t + 1, lo + 1, (j + 1) % RING)
                if lo >= 1:
                    second_product(t - 1, lo - 1, (j - 1) % RING)
                turn_hidden(t, lo, j)

            tile_loop(pe, tile_slot)
            second_product(TILES - 1, TILES - 1, RING - 1)

        @block.vector
        def _(dve):
            dve.wait_ge(weights_in, WEIGHTS)
            for w, w_rot in ((wq_sb, wq_rot), (wkv_sb, wkv_rot)):
                src = w[:, :].rearrange("p (h t d) -> p h t d", h=HEADS, t=2)
                dst = w_rot[:, :].rearrange("p (h t d) -> p h t d", h=HEADS, t=2)
                dve.tensor_copy(dst[:, :, 0], src[:, :, 1])
                dve.tensor_copy(dst[:, :, 1], src[:, :, 0]).then_inc(setup_dve, 1)
            for h in range(4):
                dve.tensor_scalar(wo_own[:, h], wo_sb[:, :], cfs("own4")[:, h:h + 1], None, ALU.mult)
                dve.tensor_scalar(wo0_own[:, h], wo0_sb[:, :], cfs("own4")[:, h:h + 1], None, ALU.mult)
            dve.tensor_copy(base[:, 1], cfs("first")).then_inc(setup_dve, 1)
            dve.memset(max_part[:, :, :], 0.0).then_inc(setup_dve, 1)
            dve.wait_ge(biases_in, 32)
            dve.tensor_copy(bias_part[:, 0], bias_in[:, :]).then_inc(setup_dve, 1)
            dve.wait_ge(setup_dve, 5)
            dve.tensor_tensor(bias_rest[:, 0], bias_in[:, :], bias_part[:, 0], ALU.subtract).then_inc(setup_dve, 1)
            dve.wait_ge(setup_dve, 6)
            dve.tensor_copy(bias_part[:, 1], bias_rest[:, 0]).then_inc(setup_dve, 1)
            dve.wait_ge(setup_dve, 7)
            dve.tensor_tensor(bias_rest[:, 1], bias_rest[:, 0], bias_part[:, 1], ALU.subtract).then_inc(setup_dve, 1)
            dve.wait_ge(setup_dve, 8)
            dve.tensor_copy(bias_part[:, 2], bias_rest[:, 1]).then_inc(setup_dve, 1)

            def turn(batch, made, turned, free, by_cos, by_sin, blo):
                dve.wait_ge(made, batch + 1)
                if blo >= 1:
                    dve.wait_ge(free, batch)
                dve.tensor_tensor(by_cos[:, :], B6[:, 0:SEQ], cfs("cos"), ALU.mult)
                dve.tensor_tensor(by_sin[:, :], B6[:, SEQ:], cfs("sin"), ALU.mult).then_inc(turned, 1)

            def row_maximum(u, c):
                dve.wait_ge(scores_made, u + 1)
                dve.tensor_reduce(row_max[:, c], S[:, 2 * c:2 * c + 2].rearrange("p a (g k) -> p (a g) k", k=SEG),
                                  AX.X, ALU.max).then_inc(max_ready, 1)

            def max_parts(u, c):
                dst = max_part[:, c].rearrange("m (s b i) -> m s b i", s=2, b=2)

                def wide(a):
                    return a[:, :].rearrange("m (s i) -> m s i", s=2).unsqueeze(2).to_broadcast([32, 2, 2, SEG])

                dve.wait_ge(max_turned, u + 1)
                dve.tensor_reduce(neg_max[:, :].rearrange("m (s i) -> m s i", s=2),
                                  B6[0:32, 0:P].rearrange("m (s b i) -> m s i b", s=2, b=2),
                                  AX.X, ALU.max, negate=True).then_inc(neg_ready, 1)
                dve.wait_ge(neg_ready, u + 1)
                dve.tensor_copy(dst[0:32], wide(neg_max)).then_inc(part1_ready, 1)
                dve.wait_ge(part1_ready, u + 1)
                dve.tensor_tensor(rest1[:, :].rearrange("m (s i) -> m s i", s=2),
                                  neg_max[:, :].rearrange("m (s i) -> m s i", s=2), dst[0:32, :, 0],
                                  ALU.subtract).then_inc(rest1_ready, 1)
                dve.wait_ge(rest1_ready, u + 1)
                dve.tensor_copy(part2[:, :], rest1[:, :])
                dve.tensor_copy(dst[32:64], wide(rest1)).then_inc(part2_ready, 1)
                dve.wait_ge(part2_ready, u + 1)
                dve.tensor_tensor(rest2[:, :], rest1[:, :], part2[:, :], ALU.subtract).then_inc(rest2_ready, 1)
                dve.wait_ge(rest2_ready, u + 1)
                dve.tensor_copy(dst[64:96], wide(rest2)).then_inc(max_parts_ready, 1)

            def divide(u, c):
                dve.wait_ge(total_made, u + 1)
                dve.reciprocal(total_sb[:, :], B7[:, 0:P]).then_inc(total_ready, 1)
                dve.wait_ge(values_made, u + 1)
                dve.wait_ge(total_ready, u + 1)
                total = total_sb[:, :].rearrange("p (r s i) -> p s r i", r=2, s=2)
                for s2 in range(2):
                    ins = dve.tensor_tensor(headed[:, c].rearrange("p h (r s i) -> p r h s i", r=2, s=2)[:, :, :, s2],
                                            O[:, s2, 0:256].rearrange("p (r h i) -> p r h i", r=2, h=4),
                                            total_sb[:, :].rearrange("p (r s i) -> p r s i", r=2, s=2)[:, :, s2].unsqueeze(2)
                                            .to_broadcast([P, 2, 4, SEG]), ALU.mult)
                ins.then_inc(headed_ready, 1)

            def choose(u, c):
                dve.wait_ge(route_made, u + 1)
                dve.tensor_tensor(score[:, :], B7[:, 0:8], br_sb[:, :], ALU.add).then_inc(score_ready, 1)
                dve.wait_ge(score_ready, u + 1)
                dve.tensor_reduce(top[:, :], score[:, :], AX.X, ALU.max).then_inc(top_ready, 1)
                dve.wait_ge(top_ready, u + 1)
                dve.scalar_tensor_tensor(out=keyed[:, :], in0=score[:, :], scalar=top[:, 0:1], in1=cfs("rev"),
                                         op0=ALU.is_ge, op1=ALU.mult).then_inc(keyed_ready, 1)
                dve.wait_ge(keyed_ready, u + 1)
                dve.tensor_reduce(ktop[:, :], keyed[:, :], AX.X, ALU.max).then_inc(ktop_ready, 1)
                dve.wait_ge(ktop_ready, u + 1)
                dve.tensor_scalar(chosen[:, c], cfs("rev"), ktop[:, 0:1], None, ALU.is_equal).then_inc(chosen_ready, 1)

            def add_residual(u, c, ring):
                dve.wait_ge(attn_made, u + 1)
                dve.wait_ge(x_bias_ready, add_residual.batch + 1)
                dve.tensor_tensor(resid[:, c], B7[:, 0:P], x_bias[:, ring], ALU.add).then_inc(resid_ready, 1)
                dve.wait_ge(resid_ready, u + 1)
                dve.bn_stats(stats[:, :], resid[:, c]).then_inc(stats_ready, 1)
                settled(dve)
                dve.wait_ge(stats_ready, u + 1)
                dve.bn_aggr(mean_var[:, c], stats[:, :]).then_inc(mv_ready, 1)

            def positions(u, c, ring, ulo):
                new, old = c, (c + 1) % 2
                dve.wait_ge(rank_made, u + 1)
                if ulo >= 1:
                    dve.wait_ge(base_ready, u)
                dve.tensor_tensor(place8[:, :], B7[:, 0:8], base[:, old], ALU.add).then_inc(place8_ready, 1)
                dve.tensor_tensor(base[:, new], B7[:, 8:16], base[:, old], ALU.add).then_inc(base_ready, 1)
                dve.wait_ge(place8_ready, u + 1)
                dve.tensor_tensor_reduce(out=place_prod[:, :], in0=place8[:, :], in1=chosen[:, c], scale=1.0, scalar=0.0,
                                         op0=ALU.mult, op1=ALU.add, accum_out=place[:, :]).then_inc(place_ready, 1)
                dve.wait_ge(place_ready, u + 1)
                if ulo >= 4:
                    dve.wait_ge(row_out[ring], positions.sent)
                dve.tensor_copy(place_i[:, ring:ring + 1], place[:, :]).then_inc(place_i_ready, 1)

            def turn_probs(u, c):
                dve.wait_ge(prob_ready, u + 1)
                dve.transpose(prob_t[:, c], prob[:, c]).then_inc(prob_t_ready, 1)

            def normalise(u, c, ring, ulo):
                dve.wait_ge(rstd_ready, u + 1)
                if ulo >= 4:
                    dve.wait_ge(row_out[ring], normalise.sent)
                dve.tensor_scalar(row[:, ring, 0:P], resid[:, c], mean_var[:, c, 0:1], rstd[:, 0:1],
                                  ALU.subtract, ALU.mult).then_inc(row_ready, 1)

            def slot(k, b, lo, hi, j):
                c = j % 2
                o = (c + 1) % 2
                max_parts(k, c)
                if lo >= 1:
                    divide(k - 1, o)
                if hi + 1 < UNITS:
                    row_maximum(k + 1, o)
                nb = b + (j + 3) // 2 if j % 2 else b + j // 2 + 1
                nlo = (lo + (3 if j % 2 else 2)) // 2
                prep = (hi + (3 if j % 2 else 2)) // 2 < BATCHES
                turn_probs(k, c)
                if prep and j % 2 == 0:
                    turn(nb, q_made, q_turned, q_ready, q_cos, q_sin, nlo)
                if lo >= 1:
                    add_residual.batch = b + (j - 1) // 2
                    add_residual(k - 1, o, (j - 1) % 4)
                if prep and j % 2:
                    turn(nb, k_made, k_turned, k_ready, k_cos, k_sin, nlo)
                if lo >= 2:
                    choose(k - 2, c)
                if lo >= 1:
                    normalise.sent = (16 * ((k - 1) // 4) if isinstance(k, int) else b * 8 + (-16 if j < 1 else 0))
                    normalise(k - 1, o, (j - 1) % 4, lo - 1)
                if lo >= 2:
                    positions.sent = (16 * ((k - 2) // 4) if isinstance(k, int) else b * 8 + (-16 if j < 2 else 0))
                    positions(k - 2, c, (j - 2) % 4, lo - 2)

            turn(0, k_made, k_turned, k_ready, k_cos, k_sin, 0)
            turn(0, q_made, q_turned, q_ready, q_cos, q_sin, 0)
            turn(1, k_made, k_turned, k_ready, k_cos, k_sin, 1)
            row_maximum(0, 0)
            unit_loop(dve, slot)
            last = UNITS - 1
            divide(last, 1)
            add_residual.batch = BATCHES - 1
            add_residual(last, 1, 3)
            choose(last - 1, 0)
            normalise.sent = 16 * (last // 4)
            normalise(last, 1, 3, last)
            positions.sent = 16 * ((last - 1) // 4)
            positions(last - 1, 0, 2, last - 1)
            choose(last, 1)
            positions.sent = 16 * (last // 4)
            positions(last, 1, 3, last)

            dve.wait_ge(base_ready, UNITS)
            fill = base[:, 1]
            dve.tensor_scalar(pad_at[:, :], fill, cfs("part"), None, ALU.add).then_inc(table_step, 1)
            dve.tensor_tensor(count8[:, :], fill[0:1], cfs("first", 1), ALU.subtract).then_inc(table_step, 1)
            dve.wait_ge(table_step, 2)
            dve.tensor_copy(pad_i[:, :], pad_at[:, :]).then_inc(pad_at_ready, 1)
            dve.tensor_tensor(over[:, :, :], count8[:, :].unsqueeze(2).to_broadcast([1, 8, 64]),
                              cfs("upto", 1).unsqueeze(1).to_broadcast([1, 8, 64]), ALU.is_gt).then_inc(table_step, 1)
            dve.wait_ge(table_step, 3)
            dve.tensor_reduce(tiles8[:, :], over[:, :, :], AX.X, ALU.add).then_inc(table_step, 1)
            dve.wait_ge(table_step, 4)
            dve.tensor_tensor(cum_prod[:, :, :], tiles8[:, :].unsqueeze(1).to_broadcast([1, 8, 8]),
                              cfs("before", 1).rearrange("p (a b) -> p a b", a=8), ALU.mult).then_inc(table_step, 1)
            dve.tensor_scalar(jump8[:, :], tiles8[:, :], -float(P), float(REGION), ALU.mult, ALU.add).then_inc(table_step, 1)
            dve.wait_ge(table_step, 6)
            dve.tensor_reduce(cum8[:, :], cum_prod[:, :, :], AX.X, ALU.add).then_inc(table_step, 1)
            dve.wait_ge(table_step, 7)
            dve.tensor_tensor(past[:, :, :], cfs("tile", 1).unsqueeze(2).to_broadcast([1, TILES, 8]),
                              cum8[:, :].unsqueeze(1).to_broadcast([1, TILES, 8]), ALU.is_ge).then_inc(table_step, 1)
            dve.wait_ge(table_step, 8)
            dve.tensor_tensor(past_jump[:, :, :], past[:, :, :], jump8[:, :].unsqueeze(1).to_broadcast([1, TILES, 8]),
                              ALU.mult).then_inc(table_step, 1)
            dve.tensor_reduce(tile_e[:, :], past[:, :, :], AX.X, ALU.add).then_inc(table_step, 1)
            dve.wait_ge(table_step, 10)
            dve.tensor_reduce(tile_j[:, :], past_jump[:, :, :], AX.X, ALU.add).then_inc(table_step, 1)
            dve.tensor_scalar(tile_e_i[:, :], tile_e[:, :], float(EXPERTS - 1), None, ALU.min).then_inc(table_step, 1)
            dve.wait_ge(table_step, 12)
            dve.scalar_tensor_tensor(out=tile_row[:, :], in0=cfs("tile", 1), scalar=float(P), in1=tile_j[:, :],
                                     op0=ALU.mult, op1=ALU.add).then_inc(table_step, 1)
            dve.wait_ge(table_step, 13)
            dve.tensor_scalar(tile_row_i[:, :], tile_row[:, :], float(EXPERTS * REGION), None, ALU.min).then_inc(table_ready, 1)

            def hidden_back(t, tlo, j):
                dve.wait_ge(hidT_made, t + 1)
                dve.tensor_copy(hidT[:, j % 2], S[:, 2 + j % 2]).then_inc(hidT_ready, 1)

            def add_back(t, r, tlo, j):
                dve.wait_ge(y_made, t + 1)
                dve.tensor_tensor(sum2[:, j % 2], O[:, j % 2, 0:P], rows_in[:, j, 0:P], ALU.add).then_inc(sum2_ready, 1)
                if tlo >= RING:
                    dve.wait_ge(tile_out[j], r * 16)
                dve.tensor_copy(token_i[:, j:j + 1], rows_in[:, j, DIM:DIM + 1]).then_inc(token_ready, 1)
                dve.wait_ge(sum2_ready, t + 1)
                dve.bn_stats(stats2[:, :], sum2[:, j % 2]).then_inc(stats2_ready, 1)
                settled(dve)
                dve.wait_ge(stats2_ready, t + 1)
                dve.bn_aggr(mv2[:, j % 2], stats2[:, :]).then_inc(mv2_ready, 1)

            def normalise2(t, j):
                dve.wait_ge(rstd2_ready, t + 1)
                dve.tensor_scalar(done_rows[:, j], sum2[:, j % 2], mv2[:, j % 2, 0:1], rstd2[:, j % 2],
                                  ALU.subtract, ALU.mult).then_inc(done_ready, 1)

            def tile_slot(t, r, lo, hi, j):
                if lo >= 2:
                    normalise2(t - 2, (j - 2) % RING)
                if lo >= 1:
                    add_back(t - 1, r - (1 if j == 0 else 0), lo - 1, (j - 1) % RING)
                hidden_back(t, lo, j)

            tile_loop(dve, tile_slot)
            normalise2(TILES - 2, RING - 2)
            add_back(TILES - 1, TILES // RING - 1, TILES - 1, RING - 1)
            normalise2(TILES - 1, RING - 1)

        @block.scalar
        def _(act):
            def copy_xT(batch, par):
                act.wait_ge(xT_made, batch + 1)
                act.copy(xT[:, par], B6[:, 0:SEQ]).then_inc(xT_ready, 1)

            def copy_v(batch, par):
                act.wait_ge(v_made, batch + 1)
                act.copy(v_win[:, par].rearrange("p a b -> p (a b)"), B6[:, :]).then_inc(v_ready, 1)

            def spread_k(batch, par, heads):
                act.wait_ge(k_ready, batch + 1)
                for h in heads:
                    ins = act.activation(k_own[:, par, h].rearrange("p (s k) -> p s k", s=8), kv_win[:, par, :, 1],
                                         ACT.Copy, scale=cfs("own8")[:, h:h + 1])
                if heads[-1] == 7:
                    ins.then_inc(k_own_ready, 1)

            def exponentials(u, c):
                act.wait_ge(shifted, u + 1)
                act.activation(prob[:, c], S[:, 2 * c:2 * c + 2].rearrange("p a n -> p (a n)"), ACT.Exp,
                               scale=SCALE).then_inc(prob_ready, 1)

            def widen_sums(u):
                act.wait_ge(key_sum_ready, u + 1)
                src = key_sum[:, :].rearrange("p (a r h) -> p r a h", a=2, r=2)
                for pair in range(2):
                    ins = act.copy(sum_wide[:, pair].rearrange("p (a h d) -> p a h d", a=2, h=8),
                                   src[:, pair].unsqueeze(3).to_broadcast([P, 2, 8, HD]))
                ins.then_inc(sum_wide_ready, 1)

            def copy_x1T(u, c):
                act.wait_ge(x1T_made, u + 1)
                act.copy(x1T[:, c], B6[:, 0:P]).then_inc(x1T_ready, 1)

            def slot(k, b, lo, hi, j):
                c = j % 2
                nb = b + (j + 3) // 2 if j % 2 else b + j // 2 + 1
                npar = ((j + 3) // 2 if j % 2 else j // 2 + 1) % 2
                prep = (hi + (3 if j % 2 else 2)) // 2 < BATCHES
                if prep and j % 2 == 0:
                    spread_k(nb, npar, range(5))
                exponentials(k, c)
                if lo >= 2:
                    copy_x1T(k - 2, c)
                if prep:
                    if j % 2:
                        copy_xT(nb, npar)
                    else:
                        copy_v(nb, npar)
                        spread_k(nb, npar, range(5, 8))
                widen_sums(k)

            copy_xT(0, 0)
            copy_v(0, 0)
            spread_k(0, 0, range(8))
            copy_xT(1, 1)
            unit_loop(act, slot)
            copy_x1T(UNITS - 2, 0)
            copy_x1T(UNITS - 1, 1)

            def copy_rows(t, j):
                act.wait_ge(rowsT_made, t + 1)
                act.copy(rowsT[:, j % 2], B6[:, 0:P]).then_inc(rowsT_ready, 1)

            def gelu(t, j):
                act.wait_ge(hid_made, t + 1)
                act.activation(hid[:, j % 2], S[:, j % 2], ACT.Gelu).then_inc(hid_ready, 1)

            copy_rows(0, 0)
            copy_rows(1, 1)
            gelu(0, 0)

            def tile_slot(t, r, lo, hi, j):
                if hi + 2 < TILES:
                    copy_rows(t + 2, j)
                if hi + 1 < TILES:
                    gelu(t + 1, (j + 1) % 2)

            tile_loop(act, tile_slot)

        @block.gpsimd
        def _(pool):
            nc.gpsimd.memset(kv_win[:, :, 0, 0], 0.0).then_inc(setup_pool, 1)
            nc.gpsimd.memset(row[:, :, :], 0.0).then_inc(setup_pool, 1)
            nc.gpsimd.memset(pad[:, :], 0.0).then_inc(setup_pool, 1)
            pool.wait_ge(weights_in, WEIGHTS)
            pool.wait_ge(setup_pool, 3)
            for i in range(4):
                nc.gpsimd.tensor_copy(row[:, i, DIM:DIM + 1], cfs("tok")[:, i:i + 1]).then_inc(token_set, 1)
            nc.gpsimd.tensor_scalar(pad[:, DIM:DIM + 1], cfs("part"), 1.0, float(TOKENS), ALU.mult, ALU.add).then_inc(setup_pool, 1)
            pool.wait_ge(setup_pool, 4)
            pool.dma_start(routed[EXPERTS * REGION:EXPERTS * REGION + P, :], pad[:, :]).then_inc(pads_out, 16)

            def add_k(batch, par):
                pool.wait_ge(k_turned, batch + 1)
                by_seg = [a[:, :].rearrange("p (s k) -> p s k", k=SEG) for a in (k_cos, k_sin)]
                nc.gpsimd.tensor_tensor(kv_win[:, par, :, 1], by_seg[0], by_seg[1], ALU.add)
                nc.gpsimd.tensor_tensor(kv_win[:, par, 1:, 0], by_seg[0][:, 0:7], by_seg[1][:, 0:7], ALU.add).then_inc(k_ready, 1)

            def add_q(batch, par):
                pool.wait_ge(q_turned, batch + 1)
                nc.gpsimd.tensor_tensor(qT[:, par], q_cos[:, :], q_sin[:, :], ALU.add).then_inc(q_ready, 1)

            def add_bias(batch, par, blo):
                pool.wait_ge(x_loaded[par], (batch // 2 + 1) * 16 if isinstance(batch, int) else batch * 8 + (8 if par else 16))
                if blo >= 2:
                    pool.wait_ge(resid_ready, add_bias.used)
                nc.gpsimd.tensor_tensor(x_bias[:, 2 * par:2 * par + 2], x_in[:, par], bo_sb[:, :, :], ALU.add).then_inc(x_bias_ready, 1)

            def sum_keys(u, c):
                src = prob[:, c].rearrange("p (g k) -> p g k", k=SEG)
                steps = [src, tree[:, :, :], tree2[:, :, :], tree3[:, :, :], tree4[:, :, :]]
                pool.wait_ge(prob_ready, u + 1)
                for n in range(4):
                    w = SEG >> (n + 1)
                    nc.gpsimd.tensor_tensor(steps[n + 1], steps[n][:, :, 0:w], steps[n][:, :, w:2 * w], ALU.add).then_inc(tree_step, 1)
                    pool.wait_ge(tree_step, u * 4 + n + 1)
                nc.gpsimd.tensor_tensor(key_sum[:, :].unsqueeze(2), tree4[:, :, 0:1], tree4[:, :, 1:2], ALU.add).then_inc(key_sum_ready, 1)

            def inverse_deviation(u, c):
                units = held(pool, u + 1)
                settled(pool)
                pool.wait_ge(mv_ready, units)
                nc.gpsimd.tensor_scalar(veps[:, :], mean_var[:, c, 1:2], 1.0, EPS, ALU.mult, ALU.add).then_inc(veps_ready, 1)
                pool.wait_ge(veps_ready, units)
                nc.gpsimd.tensor_tensor(rstd[:, :], veps[:, :], cfs("half"), ALU.pow).then_inc(rstd_ready, 1)

            def send(u, ring, ulo):
                if ulo >= 4:
                    sent = held(pool, send.sent)
                    settled(pool)
                    pool.wait_ge(row_out[ring], sent)
                    nc.gpsimd.tensor_scalar(row[:, ring, DIM:DIM + 1], row[:, ring, DIM:DIM + 1], 1.0, 4.0 * P,
                                            ALU.mult, ALU.add).then_inc(token_set, 1)
                units = held(pool, u + 1)
                settled(pool)
                pool.wait_ge(token_set, units if ulo >= 4 else 4)
                pool.wait_ge(place_i_ready, units)
                pool.wait_ge(row_ready, units)
                nc.gpsimd.indirect_dma_start(out=routed, out_offset=bass.IndirectOffsetOnAxis(ap=place_i[:, ring:ring + 1], axis=0),
                                             in_=row[:, ring], in_offset=None).then_inc(row_out[ring], 16)

            def slot(k, b, lo, hi, j):
                c = j % 2
                nb = b + (j + 3) // 2 if j % 2 else b + j // 2 + 1
                npar = ((j + 3) // 2 if j % 2 else j // 2 + 1) % 2
                prep = (hi + (3 if j % 2 else 2)) // 2 < BATCHES
                if j % 2 and hi + 1 < UNITS:
                    add_bias.used = k - 1
                    add_bias(b + (j + 1) // 2, (j + 1) // 2 % 2, (lo + 1) // 2)
                sum_keys(k, c)
                if prep:
                    if j % 2:
                        add_k(nb, npar)
                    else:
                        add_q(nb, npar)
                if lo >= 1:
                    inverse_deviation(k - 1, (c + 1) % 2)
                if lo >= 2:
                    send.sent = (16 * ((k - 2) // 4) if isinstance(k, int) else b * 8 + (-16 if j < 2 else 0))
                    send(k - 2, (j - 2) % 4, lo - 2)

            add_k(0, 0)
            add_q(0, 0)
            add_bias(0, 0, 0)
            add_k(1, 1)
            unit_loop(pool, slot)
            last = UNITS - 1
            inverse_deviation(last, 1)
            for u in (last - 1, last):
                send.sent = 16 * (u // 4)
                send(u, u % 4, u)
            pool.wait_ge(pad_at_ready, 1)
            for e in range(EXPERTS):
                nc.gpsimd.indirect_dma_start(out=routed, out_offset=bass.IndirectOffsetOnAxis(ap=pad_i[:, e:e + 1], axis=0),
                                             in_=pad[:, :], in_offset=None).then_inc(pads_out, 16)

            def inverse_deviation2(t, j):
                tiles = held(pool, t + 1)
                settled(pool)
                pool.wait_ge(mv2_ready, tiles)
                nc.gpsimd.tensor_scalar(veps2[:, :], mv2[:, j % 2, 1:2], 1.0, EPS, ALU.mult, ALU.add).then_inc(veps2_ready, 1)
                pool.wait_ge(veps2_ready, tiles)
                nc.gpsimd.tensor_tensor(rstd2[:, j % 2], veps2[:, :], cfs("half"), ALU.pow).then_inc(rstd2_ready, 1)

            def write_out(t, j):
                tiles = held(pool, t + 1)
                settled(pool)
                pool.wait_ge(done_ready, tiles)
                pool.wait_ge(token_ready, tiles)
                nc.gpsimd.indirect_dma_start(out=out_rows, out_offset=bass.IndirectOffsetOnAxis(ap=token_i[:, j:j + 1], axis=0),
                                             in_=done_rows[:, j], in_offset=None, bounds_check=TOKENS - 1,
                                             oob_is_err=False).then_inc(tile_out[j], 16)

            def tile_slot(t, r, lo, hi, j):
                if lo >= 1:
                    inverse_deviation2(t - 1, (j - 1) % RING)
                if lo >= 2:
                    write_out(t - 2, (j - 2) % RING)

            tile_loop(pool, tile_slot)
            inverse_deviation2(TILES - 1, RING - 1)
            write_out(TILES - 2, RING - 2)
            write_out(TILES - 1, RING - 1)


_INS = ["L0_attn_x", "L0_attn_Wq", "L0_attn_Wkv", "L0_attn_Wo", "L0_attn_bo", "L0_attn_Wo0", "L0_attn_bo0",
        "L0_ffn_wr", "L0_ffn_br", "L0_ffn_w1", "L0_ffn_b1", "L0_ffn_w2", "L0_ffn_b2"]


def kernel(**inputs):
    import concourse.bacc as bacc
    from concourse.bass_utils import run_bass_kernel_spmd as run

    nc = bacc.Bacc("TRN2", target_bir_lowering=False, num_devices=1)
    arrays, args = {}, []
    for name in _INS:
        arrays[f"in_{name}"] = np.ascontiguousarray(inputs[name])
    arrays["const_f32"], arrays["const_bf16"] = constants()
    for name, a in arrays.items():
        args.append(nc.dram_tensor(name, a.shape, mybir.dt.from_np(a.dtype), kind="ExternalInput").ap())
    args.append(nc.dram_tensor("out", (BATCHES, SEQ, DIM), F32, kind="ExternalOutput").ap())
    layer(nc, *args)
    r = run(nc, [arrays], core_ids=[0])
    return r.results[0]["out"]
```

```python
from contextlib import ExitStack

import numpy as np

import concourse.bass as bass
from concourse import mybir

F32 = mybir.dt.float32
BF16 = mybir.dt.bfloat16
I32 = mybir.dt.int32
ACT = mybir.ActivationFunctionType
ALU = mybir.AluOpType
AX = mybir.AxisListType

P = 128
BATCHES, SEQ, DIM = 32, 256, 128
HEADS, HD = 16, 8
SEG = 32
WIN = 2 * SEG
UNITS = BATCHES * SEQ // P
TOKENS = BATCHES * SEQ
EXPERTS, FF = 8, 512
CH = FF // P
ROW = DIM + 4
REGION = TOKENS + P
TILES = 72
RING = 8
MASKED = -1e30
EPS = 1e-5
SCALE = float(HD) ** -0.5

CF = {}
CB = {}


def _layout(table, widths):
    at = 0
    for name, w in widths:
        table[name] = (at, at + w)
        at += w
    return at


NF = _layout(CF, [("ident", P), ("cos", SEQ), ("sin", SEQ), ("own8", 8), ("own4", 4), ("pairs", WIN), ("heads", 2 * P), ("tok", 4),
                  ("rev", 8), ("first", 8), ("part", 1), ("half", 1), ("upto", 64), ("before", 64), ("tile", TILES)])
NB = _layout(CB, [("ident", P), ("mask", 2 * 512), ("pick", 2 * 512), ("below", P), ("ones", P)])


def constants():
    f = np.zeros((P, NF), np.float32)
    b = np.zeros((P, NB), np.float32)

    def put(a, table, name, v):
        lo, hi = table[name]
        a[:, lo:hi] = np.broadcast_to(v, (P, hi - lo))

    p = np.arange(P)
    put(f, CF, "ident", np.eye(P))
    inv_freq = (np.float32(1.0) / np.float32(10000.0) ** (np.arange(0, HD, 2, dtype=np.float32) / np.float32(HD)))
    angle = np.arange(SEQ, dtype=np.float32)[:, None] * inv_freq.astype(np.float32)[None, :]
    angle = np.concatenate([angle, angle], axis=-1).astype(np.float32)
    d = p % HD
    put(f, CF, "cos", np.cos(angle)[:, d].T)
    put(f, CF, "sin", (np.sin(angle)[:, d] * np.where(d < HD // 2, -1.0, 1.0)[None, :]).T)
    put(f, CF, "own8", (p[:, None] // HD % 8 == np.arange(8)[None]))
    put(f, CF, "own4", (p[:, None] // HD % 4 == np.arange(4)[None]))
    c = np.arange(WIN)
    put(f, CF, "pairs", (p[:, None] // 64 == c[None] // 32) & (p[:, None] % 32 == c[None] % 32))
    heads = np.zeros((P, 2, P), np.float32)
    for n in range(32):
        half, pair, h = n // 16, n // 8 % 2, n % 8
        heads[n, pair, (half * 8 + h) * HD:(half * 8 + h + 1) * HD] = 1.0
    put(f, CF, "heads", heads.reshape(P, -1))
    put(f, CF, "tok", p[:, None] + P * np.arange(4)[None])
    put(f, CF, "rev", 8.0 - np.arange(8)[None])
    put(f, CF, "first", REGION * np.arange(8)[None])
    put(f, CF, "part", p[:, None])
    put(f, CF, "half", -0.5)
    put(f, CF, "upto", 128.0 * np.arange(64)[None])
    e = np.arange(8)
    put(f, CF, "before", (e[None, :] <= e[:, None]).reshape(1, 64))
    put(f, CF, "tile", np.arange(TILES)[None])
    put(b, CB, "ident", np.eye(P))
    mask = np.zeros((P, 2, 2, 8, SEG), np.float32)
    block, query = p // SEG % 2, p % SEG
    key = np.arange(SEG)
    causal = (block[:, None] == 1) & (key[None, :] > query[:, None])
    mask += np.where(causal, MASKED, 0.0)[:, None, None, None, :]
    mask[:SEG, 0, 0] = MASKED
    put(b, CB, "mask", mask.reshape(P, -1))
    pick = np.zeros((4, 32, 2, 2, 8, SEG), np.float32)
    for half in range(2):
        for pair in range(2):
            for h in range(8):
                pick[:3, half * 16 + pair * 8 + h, half, pair, h] = 1.0
    put(b, CB, "pick", pick.reshape(P, -1))
    put(b, CB, "below", p[:, None] < p[None, :])
    put(b, CB, "ones", 1.0)
    return f, b.astype(mybir.dt.np(BF16))


def layer(nc, x, wq, wkv, wo, bo, wo0, bo0, wr, br, w1, b1, w2, b2, cf, cb, out):
    ctx = ExitStack()
    with ctx:
        def sb(name, shape, dt=F32):
            return ctx.enter_context(nc.sbuf_tensor(name, shape, dt))

        def psum(name, shape):
            return ctx.enter_context(nc.psum_tensor(name, shape, F32))

        def sem(name):
            return ctx.enter_context(nc.semaphore(name))

        routed = nc.dram_tensor("routed_rows", [EXPERTS * REGION + P, ROW], F32).ap()
        x_rows = x.rearrange("b (c p) d -> b p c d", p=P)
        out_rows = out.rearrange("b n d -> (b n) d")

        cf_sb, cb_sb = sb("cf_sb", [P, NF]), sb("cb_sb", [P, NB], BF16)
        wq_sb, wkv_sb, wo_sb, wo0_sb = (sb(n, [P, P]) for n in ("wq_sb", "wkv_sb", "wo_sb", "wo0_sb"))
        wo_own, wo0_own = sb("wo_own", [P, 4, P]), sb("wo0_own", [P, 4, P])
        wq_rot, wkv_rot = sb("wq_rot", [P, P]), sb("wkv_rot", [P, P])
        wr_sb, br_sb = sb("wr_sb", [P, 8]), sb("br_sb", [P, 8])
        bo_sb = sb("bo_sb", [P, 2, P])
        w1_sb = sb("w1_sb", [P, EXPERTS * FF])
        w2_sb = sb("w2_sb", [P, EXPERTS * CH * P])
        bias_in = sb("bias_in", [EXPERTS, FF + P])
        bias_rest = sb("bias_rest", [EXPERTS, 2, FF + P])
        bias_part = sb("bias_part", [EXPERTS, 3, FF + P], BF16)
        bias3 = sb("bias3", [3, EXPERTS, FF + P], BF16)

        def cfs(name, rows=P):
            lo, hi = CF[name]
            return cf_sb[0:rows, lo:hi]

        def cbs(name, rows=P):
            lo, hi = CB[name]
            return cb_sb[0:rows, lo:hi]

        ident, ident_b = cfs("ident"), cbs("ident")
        mask = cbs("mask").rearrange("p (c n) -> p c n", c=2)
        pick = cbs("pick", 96).rearrange("p (c n) -> p c n", c=2)

        x_in = sb("x_in", [P, 2, 2, P])
        x_bias = sb("x_bias", [P, 4, P])
        xT = sb("xT", [P, 2, SEQ])
        k_cos, k_sin, q_cos, q_sin = (sb(n, [P, SEQ]) for n in ("k_cos", "k_sin", "q_cos", "q_sin"))
        qT = sb("qT", [P, 2, SEQ])
        kv_win = sb("kv_win", [P, 2, 8, 2, SEG])
        k_own = sb("k_own", [P, 2, 8, SEQ])
        v_win = sb("v_win", [P, 2, 4, P])
        row_max = sb("row_max", [P, 2, 32])
        neg_max, rest1 = sb("neg_max", [32, 64]), sb("rest1", [32, 64])
        part2 = sb("part2", [32, 64], BF16)
        max_part = sb("max_part", [96, 2, P], BF16)
        prob = sb("prob", [P, 2, 1024])
        prob_t = sb("prob_t", [P, 2, 1024])
        tree = sb("tree", [P, 32, 16])
        tree2 = sb("tree2", [P, 32, 8])
        tree3 = sb("tree3", [P, 32, 4])
        tree4 = sb("tree4", [P, 32, 2])
        key_sum = sb("key_sum", [P, 32])
        inverse = sb("inverse", [32, 64])
        inverse_sb = sb("inverse_sb", [P, P])
        headed = sb("headed", [P, 2, 4, P])
        resid = sb("resid", [P, 2, P])
        stats, mean_var, veps, rstd = sb("stats", [P, 6]), sb("mean_var", [P, 2, 2]), sb("veps", [P, 1]), sb("rstd", [P, 2, 1])
        row = sb("row", [P, 4, ROW])
        x1T = sb("x1T", [P, 2, P])
        score, top, keyed, ktop = sb("score", [P, 8]), sb("top", [P, 1]), sb("keyed", [P, 8]), sb("ktop", [P, 1])
        chosen = sb("chosen", [P, 2, 8], BF16)
        base = sb("base", [P, 2, 8])
        place8, place_prod, place = sb("place8", [P, 8]), sb("place_prod", [P, 8]), sb("place", [P, 1])
        place_i = sb("place_i", [P, 4], I32)

        pad = sb("pad", [P, ROW])
        pad_at, pad_i = sb("pad_at", [P, 8]), sb("pad_i", [P, 8], I32)
        count8 = sb("count8", [1, 8])
        over, tiles8 = sb("over", [1, 8, 64]), sb("tiles8", [1, 8])
        cum_prod, cum8, jump8 = sb("cum_prod", [1, 8, 8]), sb("cum8", [1, 8]), sb("jump8", [1, 8])
        past, past_jump = sb("past", [1, TILES, 8]), sb("past_jump", [1, TILES, 8])
        tile_e, tile_j, tile_row = sb("tile_e", [1, TILES]), sb("tile_j", [1, TILES]), sb("tile_row", [1, TILES])
        tile_e_i, tile_row_i = sb("tile_e_i", [1, TILES], I32), sb("tile_row_i", [1, TILES], I32)

        rows_in = sb("rows_in", [P, RING, ROW])
        rowsT = sb("rowsT", [P, 2, P])
        hid = sb("hid", [P, 2, FF])
        hidT = sb("hidT", [P, 2, FF])
        sum2 = sb("sum2", [P, 2, P])
        stats2, mv2 = sb("stats2", [P, 6]), sb("mv2", [P, 2, 2])
        veps2, rstd2 = sb("veps2", [P, 1]), sb("rstd2", [P, 2, 1])
        done_rows = sb("done_rows", [P, RING, P])
        token_i = sb("token_i", [P, RING], I32)

        S = psum("S", [P, 4, 512])
        O = psum("O", [P, 2, 512])
        B6 = psum("B6", [P, 512])
        B7 = psum("B7", [P, 512])

        weights_in, experts_in, biases_in, bias_parts_in = sem("weights_in"), sem("experts_in"), sem("biases_in"), sem("bias_parts_in")
        x_loaded = [sem(f"x_loaded{i}") for i in range(2)]
        setup_dve, setup_pool = sem("setup_dve"), sem("setup_pool")
        xT_made, xT_ready = sem("xT_made"), sem("xT_ready")
        k_made, k_turned, k_ready, k_own_ready = sem("k_made"), sem("k_turned"), sem("k_ready"), sem("k_own_ready")
        q_made, q_turned, q_ready = sem("q_made"), sem("q_turned"), sem("q_ready")
        v_made, v_ready = sem("v_made"), sem("v_ready")
        x_bias_ready = sem("x_bias_ready")
        scores_made, max_ready, max_turned = sem("scores_made"), sem("max_ready"), sem("max_turned")
        neg_ready, part1_ready, part2_ready, max_parts_ready = (
            sem(n) for n in ("neg_ready", "part1_ready", "part2_ready", "max_parts_ready"))
        shifted, prob_ready, prob_t_ready = sem("shifted"), sem("prob_ready"), sem("prob_t_ready")
        tree_step, key_sum_ready, total_made, inverse_ready, inverse_wide, inverse_copied = (
            sem(n) for n in ("tree_step", "key_sum_ready", "total_made", "inverse_ready", "inverse_wide", "inverse_copied"))
        values_made, headed_ready = sem("values_made"), sem("headed_ready")
        attn_made, resid_ready, stats_ready, mv_ready, veps_ready, rstd_ready = (
            sem(n) for n in ("attn_made", "resid_ready", "stats_ready", "mv_ready", "veps_ready", "rstd_ready"))
        row_ready, x1T_made, x1T_ready, route_made = sem("row_ready"), sem("x1T_made"), sem("x1T_ready"), sem("route_made")
        score_ready, top_ready, keyed_ready, ktop_ready, chosen_ready = (
            sem(n) for n in ("score_ready", "top_ready", "keyed_ready", "ktop_ready", "chosen_ready"))
        rank_made, place8_ready, place_ready, place_i_ready, base_ready = (
            sem(n) for n in ("rank_made", "place8_ready", "place_ready", "place_i_ready", "base_ready"))
        token_set = sem("token_set")
        row_out = [sem(f"row_out{i}") for i in range(4)]
        table_step, table_ready, pad_at_ready, pads_out = sem("table_step"), sem("table_ready"), sem("pad_at_ready"), sem("pads_out")
        rows_loaded = [sem(f"rows_loaded{i}") for i in range(RING)]
        rowsT_made, rowsT_ready, hid_made, hid_ready, hidT_made, hidT_ready, y_made = (
            sem(n) for n in ("rowsT_made", "rowsT_ready", "hid_made", "hid_ready", "hidT_made", "hidT_ready", "y_made"))
        sum2_ready, stats2_ready, mv2_ready, veps2_ready, rstd2_ready, done_ready, token_ready = (
            sem(n) for n in ("sum2_ready", "stats2_ready", "mv2_ready", "veps2_ready", "rstd2_ready", "done_ready", "token_ready"))
        tile_out = [sem(f"tile_out{i}") for i in range(RING)]

        WEIGHTS = 16 * 11

        def held(eng, count):
            return count if isinstance(count, int) else eng.compute_val(count)

        def settled(eng):
            eng.wait_ge(setup_pool, 1)

        def unit_loop(eng, slot):
            for k in range(8):
                slot(k, k // 4 * 2, k, k, k % 4)
            with eng.Fori(2, UNITS // 4 - 1) as r:
                k0, b0 = eng.snap(r * 4), eng.snap(r * 2)
                for j in range(4):
                    slot(k0 + j, b0, 8, UNITS - 5, j)
            for j in range(4):
                k = UNITS - 4 + j
                slot(k, UNITS // 2 - 2, k, k, j)

        def tile_loop(eng, slot):
            for t in range(2 * RING):
                slot(t, t // RING, t, t, t % RING)
            with eng.Fori(2, TILES // RING - 1) as r:
                t0 = eng.snap(r * RING)
                for j in range(RING):
                    slot(t0 + j, r, 2 * RING, TILES - RING - 1, j)
            for j in range(RING):
                t = TILES - RING + j
                slot(t, TILES // RING - 1, t, t, j)

        block = ctx.enter_context(nc.Block())

        @block.sync
        def _(sp):
            sp.dma_start(cf_sb[:, :], cf).then_inc(weights_in, 16)
            sp.dma_start(x_in[:, 0], x_rows[0]).then_inc(x_loaded[0], 16)
            sp.dma_start(wq_sb[:, :], wq).then_inc(weights_in, 16)
            sp.dma_start(wkv_sb[:, :], wkv).then_inc(weights_in, 16)
            sp.dma_start(x_in[:, 1], x_rows[1]).then_inc(x_loaded[1], 16)
            sp.dma_start(cb_sb[:, :], cb).then_inc(weights_in, 16)
            sp.dma_start(wo_sb[:, :], wo).then_inc(weights_in, 16)
            sp.dma_start(wo0_sb[:, :], wo0).then_inc(weights_in, 16)
            sp.dma_start(wr_sb[:, :], wr).then_inc(weights_in, 16)
            sp.dma_start(br_sb[:, :], br.partition_broadcast(P)).then_inc(weights_in, 16)
            sp.dma_start(bo_sb[:, 1], bo.partition_broadcast(P)).then_inc(weights_in, 16)
            sp.dma_start(bo_sb[SEG:P, 0], bo.partition_broadcast(P - SEG)).then_inc(weights_in, 16)
            sp.dma_start(bo_sb[0:SEG, 0], bo0.partition_broadcast(SEG)).then_inc(weights_in, 16)
            sp.dma_start(bias_in[:, 0:FF], b1).then_inc(biases_in, 16)
            sp.dma_start(bias_in[:, FF:], b2).then_inc(biases_in, 16)
            sp.dma_start(w1_sb[:, :].rearrange("p (e f) -> p e f", e=EXPERTS), w1.rearrange("e h f -> h e f")).then_inc(experts_in, 16)
            sp.dma_start(w2_sb[:, :].rearrange("p (e c n) -> p e c n", e=EXPERTS, c=CH),
                         w2.rearrange("e (c p) n -> p e c n", p=P)).then_inc(experts_in, 16)
            sp.wait_ge(setup_dve, 9)
            for part in range(3):
                sp.dma_start(bias3[part:part + 1].rearrange("a e n -> a (e n)"),
                             bias_part[:, part, :]).then_inc(bias_parts_in, 16)

            def load(batch, par):
                sp.wait_ge(x_bias_ready, batch - 1)
                sp.wait_ge(xT_made, batch - 1)
                sp.dma_start(x_in[:, par], x_rows[bass.ds(batch, 1)].rearrange("b p c d -> (b p) c d")
                             if not isinstance(batch, int) else x_rows[batch]).then_inc(x_loaded[par], 16)

            with sp.Fori(1, BATCHES // 2) as r:
                b0 = sp.snap(r * 2)
                load(b0, 0)
                load(b0 + 1, 1)

            sp.wait_ge(table_ready, 1)
            for i in range(4):
                sp.wait_ge(row_out[i], 16 * (UNITS // 4))
            sp.wait_ge(pads_out, 16 * (EXPERTS + 1))

            def slot(t, r, lo, hi, j):
                if lo >= RING:
                    sp.wait_ge(sum2_ready, t - (RING - 1))
                    sp.wait_ge(token_ready, t - (RING - 1))
                at = sp.value_load(tile_row_i[0:1, bass.ds(t, 1)], min_val=0, max_val=EXPERTS * REGION)
                sp.dma_start(rows_in[:, j], routed[bass.ds(at, P), :]).then_inc(rows_loaded[j], 16)

            tile_loop(sp, slot)
            for i in range(RING):
                sp.wait_ge(tile_out[i], 16 * (TILES // RING))

        @block.tensor
        def _(pe):
            def turn_x(batch, par):
                pe.wait_ge(x_loaded[par], (batch // 2 + 1) * 16 if isinstance(batch, int) else batch * 8 + (8 if par else 16))
                for c in range(2):
                    mm = pe.transpose(O[:, 0, c * P:(c + 1) * P], x_in[:, par, c], ident)
                mm.then_inc(xT_made, 1)

            def project(batch, par, w, w_rot, made):
                pe.wait_ge(xT_ready, batch + 1)
                pe.matmul(B6[:, 0:SEQ], w[:, :], xT[:, par], start=True, stop=True)
                pe.matmul(B6[:, SEQ:], w_rot[:, :], xT[:, par], start=True, stop=True).then_inc(made, 1)

            def turn_v(batch, par):
                pe.wait_ge(k_ready, batch + 1)
                for pair in range(4):
                    mm = pe.transpose(B6[:, pair * P:(pair + 1) * P],
                                      kv_win[:, par, 2 * pair:2 * pair + 2].rearrange("p s b k -> p (s b k)"), ident)
                mm.then_inc(v_made, 1)

            def masks(c):
                for half in range(2):
                    pe.matmul(S[:, 2 * c + half], ident_b, mask[:, c], start=True, stop=False, skip_group_check=True)

            def scores(c, par, pair):
                for half in range(2):
                    rows = slice(64 * half, 64 * half + 64)
                    for s2 in range(2):
                        for blk in range(2):
                            s = 4 * c + 2 * pair + s2
                            if s - 1 + blk < 0:
                                continue
                            quad = 32 * (2 * s2 + blk)
                            mm = pe.matmul(S[quad:quad + 32, 2 * c + half, 256 * pair:256 * pair + 256],
                                           qT[rows, par, SEG * s:SEG * s + SEG],
                                           k_own[rows, par, :, SEG * (s - 1 + blk):SEG * (s + blk)],
                                           start=False, stop=False, skip_group_check=True)
                if pair == 1:
                    mm.then_inc(scores_made, 1)

            def shift(c, ring):
                for half in range(2):
                    mm = pe.matmul(S[:, 2 * c + half], max_part[:, ring], pick[:, half], start=False, stop=True,
                                   skip_group_check=True)
                mm.then_inc(shifted, 1)

            def slot(k, b, lo, hi, j):
                c, par = j % 2, j // 2
                nv, nx, nq = b + j // 2 + 1, b + j // 2 + 2, b + (j + 3) // 2
                prep_v = j % 2 == 0 and hi // 2 + 1 < BATCHES
                prep_x = j % 2 == 0 and hi // 2 + 2 < BATCHES
                prep_q = j % 2 == 1 and (hi + 3) // 2 < BATCHES
                pe.wait_ge(max_ready, k + 1)
                if lo >= 1:
                    if j % 2 == 0 and (hi + 2) // 2 < BATCHES:
                        pe.wait_ge(q_turned, nv + 1)
                    elif j % 2 and (hi + 3) // 2 < BATCHES:
                        pe.wait_ge(k_turned, nq + 1)
                    elif j % 2 and (hi + 1) // 2 < BATCHES:
                        pe.wait_ge(v_ready, nq)
                    else:
                        pe.wait_ge(x1T_ready, k - 3)
                if lo >= 3:
                    turn_row(k - 3, (j + 1) % 4)
                pe.transpose(B6[0:32, 0:P], row_max[:, c], ident).then_inc(max_turned, 1)
                if hi + 1 < UNITS:
                    if j % 2 == 1:
                        batches = held(pe, b + (j + 1) // 2 + 1)
                        settled(pe)
                        pe.wait_ge(q_ready, batches)
                        pe.wait_ge(k_own_ready, batches)
                    scores((c + 1) % 2, (j + 1) // 2 % 2, 0)
                if lo >= 1:
                    if lo >= 4:
                        pe.wait_ge(base_ready, k - 3)
                    spread_inverse(k - 1)
                if hi + 1 < UNITS:
                    scores((c + 1) % 2, (j + 1) // 2 % 2, 1)
                if lo >= 3:
                    pe.wait_ge(inverse_copied, k)
                    route(k - 3, (c + 1) % 2)
                pe.wait_ge(max_parts_ready, k + 1)
                shift(c, c)
                if (prep_v or prep_q) and lo >= 3:
                    pe.wait_ge(x1T_ready, k - 2)
                if prep_v:
                    turn_v(nv, (j // 2 + 1) % 2)
                if prep_x:
                    if lo >= 1:
                        pe.wait_ge(headed_ready, k)
                    turn_x(nx, j // 2 % 2)
                if prep_q:
                    project(nq, (j + 3) // 2 % 2, wq_sb, wq_rot, q_made)
                if lo >= 1:
                    output(k - 1, (c + 1) % 2, k - 2 if lo >= 3 else None)
                if hi + 2 < UNITS:
                    pe.wait_ge(prob_ready, k + 1)
                    masks(c)
                if prep_x:
                    pe.wait_ge(v_ready, nv + 1)
                    project(nx, j // 2 % 2, wkv_sb, wkv_rot, k_made)
                values(k, b, lo, j)
                if lo >= 1:
                    pe.wait_ge(resid_ready, k)
                if lo >= 3:
                    rank(k - 3, (c + 1) % 2)
                totals(k)

            def turn_row(u, ring):
                pe.wait_ge(row_ready, u + 1)
                pe.transpose(B6[:, P:2 * P], row[:, ring, 0:P], ident).then_inc(x1T_made, 1)

            def route(u, c):
                pe.wait_ge(x1T_ready, u + 1)
                pe.matmul(B7[:, P:P + 8], x1T[:, c], wr_sb[:, :], start=True, stop=True).then_inc(route_made, 1)

            def totals(u):
                pe.wait_ge(key_sum_ready, u + 1)
                pe.matmul(B7[0:32, P:P + WIN], key_sum[:, :], cfs("pairs"), start=True, stop=True).then_inc(total_made, 1)

            def spread_inverse(u):
                pe.wait_ge(inverse_ready, u + 1)
                for pair in range(2):
                    mm = pe.matmul(B7[:, 64 * pair:64 * pair + 64], cfs("heads", 32)[:, pair * P:(pair + 1) * P], inverse[:, :],
                                   start=True, stop=True)
                mm.then_inc(inverse_wide, 1)

            def values(k, b, lo, j):
                c, par = j % 2, j // 2
                probs, batches = held(pe, k + 1), held(pe, b + j // 2 + 1)
                settled(pe)
                pe.wait_ge(prob_t_ready, probs)
                if lo >= 1:
                    pe.wait_ge(headed_ready, k)
                if j % 2 == 0:
                    pe.wait_ge(v_ready, batches)
                for pair in range(2):
                    for s2 in range(2):
                        rows = slice(64 * s2, 64 * s2 + 64)
                        for g in range(4):
                            at = 512 * (g // 2) + 256 * pair + 128 * (g % 2)
                            mm = pe.matmul(O[32 * g:32 * g + 32, s2, 128 * pair:128 * pair + 128],
                                           v_win[rows, par, 2 * c + pair, 32 * g:32 * g + 32],
                                           prob_t[rows, c, at:at + 128], start=True, stop=True)
                mm.then_inc(values_made, 1)

            def output(u, c, scored):
                pe.wait_ge(headed_ready, u + 1)
                pe.wait_ge(inverse_copied, u + 1)
                if scored is not None:
                    pe.wait_ge(score_ready, scored)
                for h in range(4):
                    mm = pe.matmul(B7[:, 0:P], headed[:, c, h], wo_own[:, h], start=(h == 0), stop=(h == 3))
                if c == 0:
                    for h in range(4):
                        mm = pe.matmul(B7[0:SEG, 0:P], headed[:, c, h, 0:SEG], wo0_own[:, h], start=(h == 0), stop=(h == 3))
                mm.then_inc(attn_made, 1)

            def rank(u, c):
                pe.wait_ge(chosen_ready, u + 1)
                pe.matmul(B7[:, 0:8], cbs("below"), chosen[:, c], start=True, stop=True)
                pe.matmul(B7[:, 8:16], cbs("ones"), chosen[:, c], start=True, stop=True).then_inc(rank_made, 1)

            pe.wait_ge(weights_in, WEIGHTS)
            pe.wait_ge(setup_dve, 3)
            turn_x(0, 0)
            project(0, 0, wkv_sb, wkv_rot, k_made)
            turn_x(1, 1)
            pe.wait_ge(k_turned, 1)
            project(0, 0, wq_sb, wq_rot, q_made)
            masks(0)
            masks(1)
            pe.wait_ge(q_turned, 1)
            turn_v(0, 0)
            pe.wait_ge(v_ready, 1)
            project(1, 1, wkv_sb, wkv_rot, k_made)
            pe.wait_ge(k_own_ready, 1)
            pe.wait_ge(q_ready, 1)
            scores(0, 0, 0)
            scores(0, 0, 1)
            pe.wait_ge(k_turned, 2)
            project(1, 1, wq_sb, wq_rot, q_made)
            pe.wait_ge(q_turned, 2)
            unit_loop(pe, slot)

            last = UNITS - 1
            pe.wait_ge(base_ready, last - 2)
            spread_inverse(last)
            pe.wait_ge(inverse_copied, UNITS)
            output(last, 1, None)
            for u in (last - 2, last - 1, last):
                if u > last - 2:
                    pe.wait_ge(base_ready, u)
                else:
                    pe.wait_ge(resid_ready, UNITS)
                turn_row(u, u % 4)
                route(u, u % 2)
                rank(u, u % 2)

            ones3 = cbs("ones", 3)

            def turn_rows(t, r, tlo, j):
                pe.wait_ge(rows_loaded[j], r * 16 + 16)
                if tlo >= 2:
                    pe.wait_ge(rowsT_ready, t)
                pe.transpose(B6[:, 0:P], rows_in[:, j, 0:P], ident).then_inc(rowsT_made, 1)

            def first_product(t, tlo, j):
                e = pe.value_load(tile_e_i[0:1, bass.ds(t, 1)], min_val=0, max_val=EXPERTS - 1)
                pe.wait_ge(rowsT_ready, t + 1)
                if tlo >= 2:
                    pe.wait_ge(hid_ready, t - 1)
                pe.matmul(S[:, j % 2], ones3, b13[:, bass.ds(e * (FF + P), FF)], start=True, stop=False)
                pe.matmul(S[:, j % 2], rowsT[:, j % 2], w1_sb[:, bass.ds(e * FF, FF)], start=False, stop=True).then_inc(hid_made, 1)

            def turn_hidden(t, tlo, j):
                pe.wait_ge(hid_ready, t + 1)
                if tlo >= 2:
                    pe.wait_ge(hidT_ready, t - 1)
                for c in range(CH):
                    mm = pe.transpose(S[:, 2 + j % 2, c * P:(c + 1) * P], hid[:, j % 2, c * P:(c + 1) * P], ident)
                mm.then_inc(hidT_made, 1)

            def second_product(t, tlo, j):
                e = pe.value_load(tile_e_i[0:1, bass.ds(t, 1)], min_val=0, max_val=EXPERTS - 1)
                pe.wait_ge(hidT_ready, t + 1)
                if tlo >= 2:
                    pe.wait_ge(sum2_ready, t - 1)
                pe.matmul(O[:, j % 2, 0:P], ones3, b13[:, bass.ds(e * (FF + P) + FF, P)], start=True, stop=False)
                for c in range(CH):
                    mm = pe.matmul(O[:, j % 2, 0:P], hidT[:, j % 2, c * P:(c + 1) * P],
                                   w2_sb[:, bass.ds(e * (CH * P) + c * P, P)], start=False, stop=(c == CH - 1))
                mm.then_inc(y_made, 1)

            b13 = bias3[:, :, :].rearrange("a e n -> a (e n)")
            pe.wait_ge(table_ready, 1)
            pe.wait_ge(bias_parts_in, 48)
            pe.wait_ge(experts_in, 32)
            turn_rows(0, 0, 0, 0)
            pe.wait_ge(rowsT_ready, 1)
            turn_rows(1, 0, 1, 1)
            first_product(0, 0, 0)

            def tile_slot(t, r, lo, hi, j):
                if hi + 2 < TILES:
                    turn_rows(t + 2, r + (j + 2) // RING, lo + 2, (j + 2) % RING)
                if hi + 1 < TILES:
                    first_product(t + 1, lo + 1, (j + 1) % RING)
                if lo >= 1:
                    second_product(t - 1, lo - 1, (j - 1) % RING)
                turn_hidden(t, lo, j)

            tile_loop(pe, tile_slot)
            second_product(TILES - 1, TILES - 1, RING - 1)

        @block.vector
        def _(dve):
            dve.wait_ge(weights_in, WEIGHTS)
            for w, w_rot in ((wq_sb, wq_rot), (wkv_sb, wkv_rot)):
                src = w[:, :].rearrange("p (h t d) -> p h t d", h=HEADS, t=2)
                dst = w_rot[:, :].rearrange("p (h t d) -> p h t d", h=HEADS, t=2)
                dve.tensor_copy(dst[:, :, 0], src[:, :, 1])
                dve.tensor_copy(dst[:, :, 1], src[:, :, 0]).then_inc(setup_dve, 1)
            for h in range(4):
                dve.tensor_scalar(wo_own[:, h], wo_sb[:, :], cfs("own4")[:, h:h + 1], None, ALU.mult)
                dve.tensor_scalar(wo0_own[:, h], wo0_sb[:, :], cfs("own4")[:, h:h + 1], None, ALU.mult)
            dve.tensor_copy(base[:, 1], cfs("first")).then_inc(setup_dve, 1)
            dve.memset(max_part[:, :, :], 0.0).then_inc(setup_dve, 1)
            dve.wait_ge(biases_in, 32)
            dve.tensor_copy(bias_part[:, 0], bias_in[:, :]).then_inc(setup_dve, 1)
            dve.wait_ge(setup_dve, 5)
            dve.tensor_tensor(bias_rest[:, 0], bias_in[:, :], bias_part[:, 0], ALU.subtract).then_inc(setup_dve, 1)
            dve.wait_ge(setup_dve, 6)
            dve.tensor_copy(bias_part[:, 1], bias_rest[:, 0]).then_inc(setup_dve, 1)
            dve.wait_ge(setup_dve, 7)
            dve.tensor_tensor(bias_rest[:, 1], bias_rest[:, 0], bias_part[:, 1], ALU.subtract).then_inc(setup_dve, 1)
            dve.wait_ge(setup_dve, 8)
            dve.tensor_copy(bias_part[:, 2], bias_rest[:, 1]).then_inc(setup_dve, 1)

            def turn(batch, made, turned, free, by_cos, by_sin, blo):
                dve.wait_ge(made, batch + 1)
                if blo >= 1:
                    dve.wait_ge(free, batch)
                dve.tensor_tensor(by_cos[:, :], B6[:, 0:SEQ], cfs("cos"), ALU.mult)
                dve.tensor_tensor(by_sin[:, :], B6[:, SEQ:], cfs("sin"), ALU.mult).then_inc(turned, 1)

            def row_maximum(u, c):
                dve.wait_ge(scores_made, u + 1)
                dve.tensor_reduce(row_max[:, c], S[:, 2 * c:2 * c + 2].rearrange("p a (g k) -> p (a g) k", k=SEG),
                                  AX.X, ALU.max).then_inc(max_ready, 1)

            def max_parts(k, c, j, lo):
                dst = max_part[:, c].rearrange("m (s b i) -> m s b i", s=2, b=2)

                def by_segment(a):
                    return a[:, :].rearrange("m (s i) -> m s i", s=2)

                def wide(a):
                    return by_segment(a).unsqueeze(2).to_broadcast([32, 2, 2, SEG])

                dve.wait_ge(max_turned, k + 1)
                dve.tensor_reduce(by_segment(neg_max), B6[0:32, 0:P].rearrange("m (s b i) -> m s i b", s=2, b=2),
                                  AX.X, ALU.max, negate=True).then_inc(neg_ready, 1)
                if lo >= 2:
                    normalise.sent = (16 * ((k - 2) // 4) if isinstance(k, int) else max_parts.b * 8 + (-16 if j < 2 else 0))
                    normalise(k - 2, c, (j + 2) % 4, lo - 2)
                dve.wait_ge(neg_ready, k + 1)
                dve.tensor_copy(dst[0:32], wide(neg_max)).then_inc(part1_ready, 1)
                if lo >= 4:
                    add_places(k - 4, c)
                dve.wait_ge(part1_ready, k + 1)
                dve.tensor_tensor(by_segment(rest1), by_segment(neg_max), dst[0:32, :, 0], ALU.subtract)
                dve.tensor_tensor(by_segment(part2), by_segment(neg_max), dst[0:32, :, 0], ALU.subtract).then_inc(part2_ready, 1)
                dve.tensor_tensor(dst[32:64], wide(neg_max), dst[0:32], ALU.subtract)
                if lo >= 4:
                    pick_place(k - 4, c)
                dve.wait_ge(part2_ready, k + 1)
                dve.tensor_tensor(dst[64:96], wide(rest1), wide(part2), ALU.subtract).then_inc(max_parts_ready, 1)
                if lo >= 4:
                    positions.sent = (16 * ((k - 4) // 4) if isinstance(k, int) else max_parts.b * 8 - 16)
                    positions(k - 4, j % 4, lo - 4)

            def invert(u):
                dve.wait_ge(total_made, u + 1)
                dve.reciprocal(inverse[:, :], B7[0:32, P:P + WIN]).then_inc(inverse_ready, 1)

            def divide(u, c, s2):
                if s2 == 0:
                    dve.wait_ge(inverse_copied, u + 1)
                    dve.wait_ge(values_made, u + 1)
                ins = dve.tensor_tensor(headed[:, c].rearrange("p h (r s i) -> p r h s i", r=2, s=2)[:, :, :, s2],
                                        O[:, s2, 0:256].rearrange("p (r h i) -> p r h i", r=2, h=4),
                                        inverse_sb[:, :].rearrange("p (r s i) -> p r s i", r=2, s=2)[:, :, s2].unsqueeze(2)
                                        .to_broadcast([P, 2, 4, SEG]), ALU.mult)
                if s2 == 1:
                    ins.then_inc(headed_ready, 1)

            def add_score(u):
                dve.wait_ge(route_made, u + 1)
                dve.tensor_tensor(score[:, :], B7[:, P:P + 8], br_sb[:, :], ALU.add).then_inc(score_ready, 1)

            def top_score(u):
                dve.wait_ge(score_ready, u + 1)
                dve.tensor_reduce(top[:, :], score[:, :], AX.X, ALU.max).then_inc(top_ready, 1)

            def key_experts(u):
                dve.wait_ge(top_ready, u + 1)
                dve.scalar_tensor_tensor(out=keyed[:, :], in0=score[:, :], scalar=top[:, 0:1], in1=cfs("rev"),
                                         op0=ALU.is_ge, op1=ALU.mult).then_inc(keyed_ready, 1)

            def top_key(u):
                dve.wait_ge(keyed_ready, u + 1)
                dve.tensor_reduce(ktop[:, :], keyed[:, :], AX.X, ALU.max).then_inc(ktop_ready, 1)

            def one_hot(u, c):
                dve.wait_ge(ktop_ready, u + 1)
                dve.tensor_scalar(chosen[:, c], cfs("rev"), ktop[:, 0:1], None, ALU.is_equal).then_inc(chosen_ready, 1)

            def add_residual(u, c, ring):
                dve.wait_ge(attn_made, u + 1)
                dve.wait_ge(x_bias_ready, add_residual.batch + 1)
                dve.tensor_tensor(resid[:, c], B7[:, 0:P], x_bias[:, ring], ALU.add).then_inc(resid_ready, 1)

            def deviation_parts(u, c):
                dve.wait_ge(resid_ready, u + 1)
                dve.bn_stats(stats[:, :], resid[:, c]).then_inc(stats_ready, 1)

            def deviation(u, c):
                settled(dve)
                dve.wait_ge(stats_ready, u + 1)
                dve.bn_aggr(mean_var[:, c], stats[:, :]).then_inc(mv_ready, 1)

            def add_places(u, c):
                new, old = c, (c + 1) % 2
                dve.wait_ge(rank_made, u + 1)
                if not isinstance(u, int) or u >= 1:
                    dve.wait_ge(base_ready, u)
                dve.tensor_tensor(place8[:, :], B7[:, 0:8], base[:, old], ALU.add).then_inc(place8_ready, 1)
                dve.tensor_tensor(base[:, new], B7[:, 8:16], base[:, old], ALU.add).then_inc(base_ready, 1)

            def pick_place(u, c):
                dve.wait_ge(place8_ready, u + 1)
                dve.tensor_tensor_reduce(out=place_prod[:, :], in0=place8[:, :], in1=chosen[:, c], scale=1.0, scalar=0.0,
                                         op0=ALU.mult, op1=ALU.add, accum_out=place[:, :]).then_inc(place_ready, 1)

            def positions(u, ring, ulo):
                dve.wait_ge(place_ready, u + 1)
                if ulo >= 4:
                    dve.wait_ge(row_out[ring], positions.sent)
                dve.tensor_copy(place_i[:, ring:ring + 1], place[:, :]).then_inc(place_i_ready, 1)

            def turn_probs(u, c):
                dve.wait_ge(prob_ready, u + 1)
                dve.transpose(prob_t[:, c], prob[:, c]).then_inc(prob_t_ready, 1)

            def normalise(u, c, ring, ulo):
                dve.wait_ge(rstd_ready, u + 1)
                if ulo >= 4:
                    dve.wait_ge(row_out[ring], normalise.sent)
                dve.tensor_scalar(row[:, ring, 0:P], resid[:, c], mean_var[:, c, 0:1], rstd[:, c],
                                  ALU.subtract, ALU.mult).then_inc(row_ready, 1)

            def slot(k, b, lo, hi, j):
                c = j % 2
                o = (c + 1) % 2
                nv, nx, nq = b + j // 2 + 1, b + j // 2 + 2, b + (j + 3) // 2
                prep_v = j % 2 == 0 and hi // 2 + 1 < BATCHES
                prep_x = j % 2 == 0 and hi // 2 + 2 < BATCHES
                prep_q = j % 2 == 1 and (hi + 3) // 2 < BATCHES
                max_parts.b = b
                max_parts(k, c, j, lo)
                if lo >= 1:
                    divide(k - 1, o, 0)
                    divide(k - 1, o, 1)
                if lo >= 3:
                    add_score(k - 3)
                if hi + 1 < UNITS:
                    row_maximum(k + 1, o)
                if lo >= 3:
                    top_score(k - 3)
                turn_probs(k, c)
                if lo >= 3:
                    key_experts(k - 3)
                if lo >= 1:
                    add_residual.batch = b + (j - 1) // 2
                    add_residual(k - 1, o, (j - 1) % 4)
                if lo >= 3:
                    top_key(k - 3)
                if lo >= 1:
                    deviation_parts(k - 1, o)
                if lo >= 3:
                    one_hot(k - 3, o)
                if lo >= 1:
                    deviation(k - 1, o)
                if prep_x:
                    turn(nx, k_made, k_turned, k_ready, k_cos, k_sin, 2)
                if prep_q:
                    turn(nq, q_made, q_turned, q_ready, q_cos, q_sin, 2)
                invert(k)

            turn(0, k_made, k_turned, k_ready, k_cos, k_sin, 0)
            turn(0, q_made, q_turned, q_ready, q_cos, q_sin, 0)
            turn(1, k_made, k_turned, k_ready, k_cos, k_sin, 1)
            row_maximum(0, 0)
            turn(1, q_made, q_turned, q_ready, q_cos, q_sin, 1)
            unit_loop(dve, slot)
            last = UNITS - 1

            def places(u):
                add_places(u, u % 2)
                pick_place(u, u % 2)
                positions.sent = 16 * (u // 4)
                positions(u, u % 4, u)

            normalise.sent = 16 * (last // 4)
            normalise(last - 1, 0, 2, last - 1)
            places(last - 3)
            divide(last, 1, 0)
            divide(last, 1, 1)
            add_residual.batch = BATCHES - 1
            add_residual(last, 1, 3)
            deviation_parts(last, 1)
            deviation(last, 1)
            for u in (last - 2, last - 1, last):
                add_score(u)
                top_score(u)
                key_experts(u)
                top_key(u)
                one_hot(u, u % 2)
                if u == last - 2:
                    normalise(last, 1, 3, last)
                places(u)

            dve.wait_ge(base_ready, UNITS)
            fill = base[:, 1]
            dve.tensor_scalar(pad_at[:, :], fill, cfs("part"), None, ALU.add).then_inc(table_step, 1)
            dve.tensor_tensor(count8[:, :], fill[0:1], cfs("first", 1), ALU.subtract).then_inc(table_step, 1)
            dve.wait_ge(table_step, 2)
            dve.tensor_copy(pad_i[:, :], pad_at[:, :]).then_inc(pad_at_ready, 1)
            dve.tensor_tensor(over[:, :, :], count8[:, :].unsqueeze(2).to_broadcast([1, 8, 64]),
                              cfs("upto", 1).unsqueeze(1).to_broadcast([1, 8, 64]), ALU.is_gt).then_inc(table_step, 1)
            dve.wait_ge(table_step, 3)
            dve.tensor_reduce(tiles8[:, :], over[:, :, :], AX.X, ALU.add).then_inc(table_step, 1)
            dve.wait_ge(table_step, 4)
            dve.tensor_tensor(cum_prod[:, :, :], tiles8[:, :].unsqueeze(1).to_broadcast([1, 8, 8]),
                              cfs("before", 1).rearrange("p (a b) -> p a b", a=8), ALU.mult).then_inc(table_step, 1)
            dve.tensor_scalar(jump8[:, :], tiles8[:, :], -float(P), float(REGION), ALU.mult, ALU.add).then_inc(table_step, 1)
            dve.wait_ge(table_step, 6)
            dve.tensor_reduce(cum8[:, :], cum_prod[:, :, :], AX.X, ALU.add).then_inc(table_step, 1)
            dve.wait_ge(table_step, 7)
            dve.tensor_tensor(past[:, :, :], cfs("tile", 1).unsqueeze(2).to_broadcast([1, TILES, 8]),
                              cum8[:, :].unsqueeze(1).to_broadcast([1, TILES, 8]), ALU.is_ge).then_inc(table_step, 1)
            dve.wait_ge(table_step, 8)
            dve.tensor_tensor(past_jump[:, :, :], past[:, :, :], jump8[:, :].unsqueeze(1).to_broadcast([1, TILES, 8]),
                              ALU.mult).then_inc(table_step, 1)
            dve.tensor_reduce(tile_e[:, :], past[:, :, :], AX.X, ALU.add).then_inc(table_step, 1)
            dve.wait_ge(table_step, 10)
            dve.tensor_reduce(tile_j[:, :], past_jump[:, :, :], AX.X, ALU.add).then_inc(table_step, 1)
            dve.tensor_scalar(tile_e_i[:, :], tile_e[:, :], float(EXPERTS - 1), None, ALU.min).then_inc(table_step, 1)
            dve.wait_ge(table_step, 12)
            dve.scalar_tensor_tensor(out=tile_row[:, :], in0=cfs("tile", 1), scalar=float(P), in1=tile_j[:, :],
                                     op0=ALU.mult, op1=ALU.add).then_inc(table_step, 1)
            dve.wait_ge(table_step, 13)
            dve.tensor_scalar(tile_row_i[:, :], tile_row[:, :], float(EXPERTS * REGION), None, ALU.min).then_inc(table_ready, 1)

            def hidden_back(t, tlo, j):
                dve.wait_ge(hidT_made, t + 1)
                dve.tensor_copy(hidT[:, j % 2], S[:, 2 + j % 2]).then_inc(hidT_ready, 1)

            def add_back(t, r, tlo, j):
                dve.wait_ge(y_made, t + 1)
                dve.tensor_tensor(sum2[:, j % 2], O[:, j % 2, 0:P], rows_in[:, j, 0:P], ALU.add).then_inc(sum2_ready, 1)
                if tlo >= RING:
                    dve.wait_ge(tile_out[j], r * 16)
                dve.tensor_copy(token_i[:, j:j + 1], rows_in[:, j, DIM:DIM + 1]).then_inc(token_ready, 1)
                dve.wait_ge(sum2_ready, t + 1)
                dve.bn_stats(stats2[:, :], sum2[:, j % 2]).then_inc(stats2_ready, 1)
                settled(dve)
                dve.wait_ge(stats2_ready, t + 1)
                dve.bn_aggr(mv2[:, j % 2], stats2[:, :]).then_inc(mv2_ready, 1)

            def normalise2(t, j):
                dve.wait_ge(rstd2_ready, t + 1)
                dve.tensor_scalar(done_rows[:, j], sum2[:, j % 2], mv2[:, j % 2, 0:1], rstd2[:, j % 2],
                                  ALU.subtract, ALU.mult).then_inc(done_ready, 1)

            def tile_slot(t, r, lo, hi, j):
                if lo >= 2:
                    normalise2(t - 2, (j - 2) % RING)
                if lo >= 1:
                    add_back(t - 1, r - (1 if j == 0 else 0), lo - 1, (j - 1) % RING)
                hidden_back(t, lo, j)

            tile_loop(dve, tile_slot)
            normalise2(TILES - 2, RING - 2)
            add_back(TILES - 1, TILES // RING - 1, TILES - 1, RING - 1)
            normalise2(TILES - 1, RING - 1)

        @block.scalar
        def _(act):
            def copy_xT(batch, par):
                act.wait_ge(xT_made, batch + 1)
                act.copy(xT[:, par], O[:, 0, 0:SEQ]).then_inc(xT_ready, 1)

            def copy_v(batch, par):
                act.wait_ge(v_made, batch + 1)
                act.copy(v_win[:, par].rearrange("p a b -> p (a b)"), B6[:, :]).then_inc(v_ready, 1)

            def spread_k(batch, par, heads):
                act.wait_ge(k_ready, batch + 1)
                for h in heads:
                    ins = act.activation(k_own[:, par, h].rearrange("p (s k) -> p s k", s=8), kv_win[:, par, :, 1],
                                         ACT.Copy, scale=cfs("own8")[:, h:h + 1])
                if heads[-1] == 7:
                    ins.then_inc(k_own_ready, 1)

            def exponentials(u, c):
                act.wait_ge(shifted, u + 1)
                act.activation(prob[:, c], S[:, 2 * c:2 * c + 2].rearrange("p a n -> p (a n)"), ACT.Exp,
                               scale=SCALE).then_inc(prob_ready, 1)

            def copy_x1T(u, c, read):
                act.wait_ge(x1T_made, u + 1)
                if read is not None:
                    act.wait_ge(neg_ready, read)
                act.copy(x1T[:, c], B6[:, P:2 * P]).then_inc(x1T_ready, 1)

            def copy_inverse(u):
                act.wait_ge(inverse_wide, u + 1)
                act.copy(inverse_sb[:, :], B7[:, 0:P]).then_inc(inverse_copied, 1)

            def slot(k, b, lo, hi, j):
                c = j % 2
                nv, nx, nq = b + j // 2 + 1, b + j // 2 + 2, b + (j + 3) // 2
                prep_v = j % 2 == 0 and hi // 2 + 1 < BATCHES
                prep_x = j % 2 == 0 and hi // 2 + 2 < BATCHES
                prep_q = j % 2 == 1 and (hi + 3) // 2 < BATCHES
                if lo >= 3:
                    copy_x1T(k - 3, (c + 1) % 2, k + 1)
                if lo >= 1:
                    copy_inverse(k - 1)
                if prep_q:
                    spread_k(nq, (j + 3) // 2 % 2, range(5))
                exponentials(k, c)
                if prep_v:
                    copy_v(nv, (j // 2 + 1) % 2)
                if prep_x:
                    copy_xT(nx, j // 2 % 2)
                if prep_q:
                    spread_k(nq, (j + 3) // 2 % 2, range(5, 8))

            copy_xT(0, 0)
            copy_xT(1, 1)
            copy_v(0, 0)
            spread_k(0, 0, range(8))
            spread_k(1, 1, range(8))
            unit_loop(act, slot)
            copy_inverse(UNITS - 1)
            for u in range(UNITS - 3, UNITS):
                copy_x1T(u, u % 2, None)

            def copy_rows(t, j):
                act.wait_ge(rowsT_made, t + 1)
                act.copy(rowsT[:, j % 2], B6[:, 0:P]).then_inc(rowsT_ready, 1)

            def gelu(t, j):
                act.wait_ge(hid_made, t + 1)
                act.activation(hid[:, j % 2], S[:, j % 2], ACT.Gelu).then_inc(hid_ready, 1)

            copy_rows(0, 0)
            copy_rows(1, 1)
            gelu(0, 0)

            def tile_slot(t, r, lo, hi, j):
                if hi + 2 < TILES:
                    copy_rows(t + 2, j)
                if hi + 1 < TILES:
                    gelu(t + 1, (j + 1) % 2)

            tile_loop(act, tile_slot)

        @block.gpsimd
        def _(pool):
            nc.gpsimd.memset(kv_win[:, :, 0, 0], 0.0).then_inc(setup_pool, 1)
            nc.gpsimd.memset(row[:, :, :], 0.0).then_inc(setup_pool, 1)
            nc.gpsimd.memset(pad[:, :], 0.0).then_inc(setup_pool, 1)
            pool.wait_ge(weights_in, WEIGHTS)
            pool.wait_ge(setup_pool, 3)
            for i in range(4):
                nc.gpsimd.tensor_copy(row[:, i, DIM:DIM + 1], cfs("tok")[:, i:i + 1]).then_inc(token_set, 1)
            nc.gpsimd.tensor_scalar(pad[:, DIM:DIM + 1], cfs("part"), 1.0, float(TOKENS), ALU.mult, ALU.add).then_inc(setup_pool, 1)
            pool.wait_ge(setup_pool, 4)
            pool.dma_start(routed[EXPERTS * REGION:EXPERTS * REGION + P, :], pad[:, :]).then_inc(pads_out, 16)

            def add_k(batch, par):
                pool.wait_ge(k_turned, batch + 1)
                by_seg = [a[:, :].rearrange("p (s k) -> p s k", k=SEG) for a in (k_cos, k_sin)]
                nc.gpsimd.tensor_tensor(kv_win[:, par, :, 1], by_seg[0], by_seg[1], ALU.add)
                nc.gpsimd.tensor_tensor(kv_win[:, par, 1:, 0], by_seg[0][:, 0:7], by_seg[1][:, 0:7], ALU.add).then_inc(k_ready, 1)

            def add_q(batch, par):
                pool.wait_ge(q_turned, batch + 1)
                nc.gpsimd.tensor_tensor(qT[:, par], q_cos[:, :], q_sin[:, :], ALU.add).then_inc(q_ready, 1)

            def add_bias(batch, par, blo):
                pool.wait_ge(x_loaded[par], (batch // 2 + 1) * 16 if isinstance(batch, int) else batch * 8 + (8 if par else 16))
                if blo >= 2:
                    pool.wait_ge(resid_ready, add_bias.used)
                nc.gpsimd.tensor_tensor(x_bias[:, 2 * par:2 * par + 2], x_in[:, par], bo_sb[:, :, :], ALU.add).then_inc(x_bias_ready, 1)

            def sum_keys(u, c):
                src = prob[:, c].rearrange("p (g k) -> p g k", k=SEG)
                steps = [src, tree[:, :, :], tree2[:, :, :], tree3[:, :, :], tree4[:, :, :]]
                pool.wait_ge(prob_ready, u + 1)
                for n in range(4):
                    w = SEG >> (n + 1)
                    nc.gpsimd.tensor_tensor(steps[n + 1], steps[n][:, :, 0:w], steps[n][:, :, w:2 * w], ALU.add).then_inc(tree_step, 1)
                    pool.wait_ge(tree_step, u * 4 + n + 1)
                nc.gpsimd.tensor_tensor(key_sum[:, :].unsqueeze(2), tree4[:, :, 0:1], tree4[:, :, 1:2], ALU.add).then_inc(key_sum_ready, 1)

            def inverse_deviation(u, c):
                units = held(pool, u + 1)
                settled(pool)
                pool.wait_ge(mv_ready, units)
                nc.gpsimd.tensor_scalar(veps[:, :], mean_var[:, c, 1:2], 1.0, EPS, ALU.mult, ALU.add).then_inc(veps_ready, 1)
                pool.wait_ge(veps_ready, units)
                nc.gpsimd.tensor_tensor(rstd[:, c], veps[:, :], cfs("half"), ALU.pow).then_inc(rstd_ready, 1)

            def send(u, ring, ulo):
                if ulo >= 4:
                    sent = held(pool, send.sent)
                    settled(pool)
                    pool.wait_ge(row_out[ring], sent)
                    nc.gpsimd.tensor_scalar(row[:, ring, DIM:DIM + 1], row[:, ring, DIM:DIM + 1], 1.0, 4.0 * P,
                                            ALU.mult, ALU.add).then_inc(token_set, 1)
                units = held(pool, u + 1)
                settled(pool)
                pool.wait_ge(token_set, units if ulo >= 4 else 4)
                pool.wait_ge(place_i_ready, units)
                pool.wait_ge(row_ready, units)
                nc.gpsimd.indirect_dma_start(out=routed, out_offset=bass.IndirectOffsetOnAxis(ap=place_i[:, ring:ring + 1], axis=0),
                                             in_=row[:, ring], in_offset=None).then_inc(row_out[ring], 16)

            def slot(k, b, lo, hi, j):
                c = j % 2
                nv, nx, nq = b + j // 2 + 1, b + j // 2 + 2, b + (j + 3) // 2
                prep_v = j % 2 == 0 and hi // 2 + 1 < BATCHES
                prep_x = j % 2 == 0 and hi // 2 + 2 < BATCHES
                prep_q = j % 2 == 1 and (hi + 3) // 2 < BATCHES
                if j % 2 and hi + 1 < UNITS:
                    add_bias.used = k - 1
                    add_bias(b + (j + 1) // 2, (j + 1) // 2 % 2, (lo + 1) // 2)
                if lo >= 4:
                    send.sent = (16 * ((k - 4) // 4) if isinstance(k, int) else b * 8 - 16)
                    send(k - 4, j % 4, lo - 4)
                sum_keys(k, c)
                if lo >= 1:
                    inverse_deviation(k - 1, (c + 1) % 2)
                if prep_x:
                    add_k(nx, j // 2 % 2)
                if prep_q:
                    add_q(nq, (j + 3) // 2 % 2)

            add_k(0, 0)
            add_q(0, 0)
            add_bias(0, 0, 0)
            add_k(1, 1)
            add_q(1, 1)
            unit_loop(pool, slot)
            last = UNITS - 1
            inverse_deviation(last, 1)
            for u in range(last - 3, UNITS):
                send.sent = 16 * (u // 4)
                send(u, u % 4, u)
            pool.wait_ge(pad_at_ready, 1)
            for e in range(EXPERTS):
                nc.gpsimd.indirect_dma_start(out=routed, out_offset=bass.IndirectOffsetOnAxis(ap=pad_i[:, e:e + 1], axis=0),
                                             in_=pad[:, :], in_offset=None).then_inc(pads_out, 16)

            def inverse_deviation2(t, j):
                tiles = held(pool, t + 1)
                settled(pool)
                pool.wait_ge(mv2_ready, tiles)
                nc.gpsimd.tensor_scalar(veps2[:, :], mv2[:, j % 2, 1:2], 1.0, EPS, ALU.mult, ALU.add).then_inc(veps2_ready, 1)
                pool.wait_ge(veps2_ready, tiles)
                nc.gpsimd.tensor_tensor(rstd2[:, j % 2], veps2[:, :], cfs("half"), ALU.pow).then_inc(rstd2_ready, 1)

            def write_out(t, j):
                tiles = held(pool, t + 1)
                settled(pool)
                pool.wait_ge(done_ready, tiles)
                pool.wait_ge(token_ready, tiles)
                nc.gpsimd.indirect_dma_start(out=out_rows, out_offset=bass.IndirectOffsetOnAxis(ap=token_i[:, j:j + 1], axis=0),
                                             in_=done_rows[:, j], in_offset=None, bounds_check=TOKENS - 1,
                                             oob_is_err=False).then_inc(tile_out[j], 16)

            def tile_slot(t, r, lo, hi, j):
                if lo >= 1:
                    inverse_deviation2(t - 1, (j - 1) % RING)
                if lo >= 2:
                    write_out(t - 2, (j - 2) % RING)

            tile_loop(pool, tile_slot)
            inverse_deviation2(TILES - 1, RING - 1)
            write_out(TILES - 2, RING - 2)
            write_out(TILES - 1, RING - 1)


_INS = ["L0_attn_x", "L0_attn_Wq", "L0_attn_Wkv", "L0_attn_Wo", "L0_attn_bo", "L0_attn_Wo0", "L0_attn_bo0",
        "L0_ffn_wr", "L0_ffn_br", "L0_ffn_w1", "L0_ffn_b1", "L0_ffn_w2", "L0_ffn_b2"]


def kernel(**inputs):
    import concourse.bacc as bacc
    from concourse.bass_utils import run_bass_kernel_spmd as run

    nc = bacc.Bacc("TRN2", target_bir_lowering=False, num_devices=1)
    arrays, args = {}, []
    for name in _INS:
        arrays[f"in_{name}"] = np.ascontiguousarray(inputs[name])
    arrays["const_f32"], arrays["const_bf16"] = constants()
    for name, a in arrays.items():
        args.append(nc.dram_tensor(name, a.shape, mybir.dt.from_np(a.dtype), kind="ExternalInput").ap())
    args.append(nc.dram_tensor("out", (BATCHES, SEQ, DIM), F32, kind="ExternalOutput").ap())
    layer(nc, *args)
    r = run(nc, [arrays], core_ids=[0])
    return r.results[0]["out"]
```

```python
from contextlib import ExitStack

import numpy as np

import concourse.bass as bass
from concourse import mybir

F32 = mybir.dt.float32
BF16 = mybir.dt.bfloat16
I32 = mybir.dt.int32
ACT = mybir.ActivationFunctionType
ALU = mybir.AluOpType
AX = mybir.AxisListType

P = 128
BATCHES, SEQ, DIM = 32, 256, 128
HEADS, HD = 16, 8
SEG = 32
WIN = 2 * SEG
UNITS = BATCHES * SEQ // P
TOKENS = BATCHES * SEQ
EXPERTS, FF = 8, 512
CH = FF // P
ROW = DIM + 4
REGION = TOKENS + P
TILES = 72
RING = 8
MASKED = -1e30
EPS = 1e-5
SCALE = float(HD) ** -0.5

CF = {}
CB = {}


def _layout(table, widths):
    at = 0
    for name, w in widths:
        table[name] = (at, at + w)
        at += w
    return at


NF = _layout(CF, [("ident", P), ("cos", SEQ), ("sin", SEQ), ("own2", 2), ("own16", HEADS), ("pairs", WIN), ("heads", 2 * P), ("tok", 4),
                  ("rev", 8), ("first", 8), ("part", 1), ("half", 1), ("upto", 64), ("before", 64), ("tile", TILES)])
NB = _layout(CB, [("ident", P), ("mask", 2 * 512), ("pick", 2 * 512), ("below", P), ("ones", P)])


def constants():
    f = np.zeros((P, NF), np.float32)
    b = np.zeros((P, NB), np.float32)

    def put(a, table, name, v):
        lo, hi = table[name]
        a[:, lo:hi] = np.broadcast_to(v, (P, hi - lo))

    p = np.arange(P)
    put(f, CF, "ident", np.eye(P))
    inv_freq = (np.float32(1.0) / np.float32(10000.0) ** (np.arange(0, HD, 2, dtype=np.float32) / np.float32(HD)))
    angle = np.arange(SEQ, dtype=np.float32)[:, None] * inv_freq.astype(np.float32)[None, :]
    angle = np.concatenate([angle, angle], axis=-1).astype(np.float32)
    d = p % HD
    put(f, CF, "cos", np.cos(angle)[:, d].T)
    put(f, CF, "sin", (np.sin(angle)[:, d] * np.where(d < HD // 2, 1.0, -1.0)[None, :]).T)
    put(f, CF, "own16", (p[:, None] // HD == np.arange(HEADS)[None]))
    put(f, CF, "own2", (p[:, None] // HD % 2 == np.arange(2)[None]))
    c = np.arange(WIN)
    put(f, CF, "pairs", (p[:, None] // 64 == c[None] // 32) & (p[:, None] % 32 == c[None] % 32))
    heads = np.zeros((P, 2, P), np.float32)
    for n in range(32):
        pair, h = n // HEADS, n % HEADS
        heads[n, pair, h * HD:(h + 1) * HD] = 1.0
    put(f, CF, "heads", heads.reshape(P, -1))
    put(f, CF, "tok", p[:, None] + P * np.arange(4)[None])
    put(f, CF, "rev", 8.0 - np.arange(8)[None])
    put(f, CF, "first", REGION * np.arange(8)[None])
    put(f, CF, "part", p[:, None])
    put(f, CF, "half", -0.5)
    put(f, CF, "upto", 128.0 * np.arange(64)[None])
    e = np.arange(8)
    put(f, CF, "before", (e[None, :] <= e[:, None]).reshape(1, 64))
    put(f, CF, "tile", np.arange(TILES)[None])
    put(b, CB, "ident", np.eye(P))
    mask = np.zeros((P, 2, HEADS, SEG), np.float32)
    block, query = p // SEG % 2, p % SEG
    key = np.arange(SEG)
    causal = (block[:, None] == 1) & (key[None, :] > query[:, None])
    mask += np.where(causal, MASKED, 0.0)[:, None, None, :]
    mask[:SEG, 0] = MASKED
    put(b, CB, "mask", mask.reshape(P, -1))
    pick = np.zeros((4, 32, 2, HEADS, SEG), np.float32)
    for pair in range(2):
        for h in range(HEADS):
            pick[:3, pair * HEADS + h, pair, h] = 1.0
    put(b, CB, "pick", pick.reshape(P, -1))
    put(b, CB, "below", p[:, None] < p[None, :])
    put(b, CB, "ones", 1.0)
    return f, b.astype(mybir.dt.np(BF16))


def layer(nc, x, wq, wkv, wo, bo, wo0, bo0, wr, br, w1, b1, w2, b2, cf, cb, out):
    ctx = ExitStack()
    with ctx:
        def sb(name, shape, dt=F32):
            return ctx.enter_context(nc.sbuf_tensor(name, shape, dt))

        def psum(name, shape):
            return ctx.enter_context(nc.psum_tensor(name, shape, F32))

        def sem(name):
            return ctx.enter_context(nc.semaphore(name))

        routed = nc.dram_tensor("routed_rows", [EXPERTS * REGION + P, ROW], F32).ap()
        x_rows = x.rearrange("b (c p) d -> b p c d", p=P)
        out_rows = out.rearrange("b n d -> (b n) d")

        cf_sb, cb_sb = sb("cf_sb", [P, NF]), sb("cb_sb", [P, NB], BF16)
        wq_sb, wkv_sb, wo_sb, wo0_sb = (sb(n, [P, P]) for n in ("wq_sb", "wkv_sb", "wo_sb", "wo0_sb"))
        wo_own, wo0_own = sb("wo_own", [P, 2, P]), sb("wo0_own", [P, 2, P])
        wr_sb, br_sb = sb("wr_sb", [P, 8]), sb("br_sb", [P, 8])
        bo_sb = sb("bo_sb", [P, 2, P])
        w1_sb = sb("w1_sb", [P, EXPERTS * FF])
        w2_sb = sb("w2_sb", [P, EXPERTS * CH * P])
        bias_in = sb("bias_in", [EXPERTS, FF + P])
        bias_rest = sb("bias_rest", [EXPERTS, 2, FF + P])
        bias_part = sb("bias_part", [EXPERTS, 3, FF + P], BF16)
        bias3 = sb("bias3", [3, EXPERTS, FF + P], BF16)

        def cfs(name, rows=P):
            lo, hi = CF[name]
            return cf_sb[0:rows, lo:hi]

        def cbs(name, rows=P):
            lo, hi = CB[name]
            return cb_sb[0:rows, lo:hi]

        ident, ident_b = cfs("ident"), cbs("ident")
        mask = cbs("mask").rearrange("p (c n) -> p c n", c=2)
        pick = cbs("pick", 96).rearrange("p (c n) -> p c n", c=2)

        x_in = sb("x_in", [P, 2, 2, P])
        x_bias = sb("x_bias", [P, 4, P])
        xT = sb("xT", [P, 2, SEQ])
        k_cos, k_sin, q_cos, q_sin = (sb(n, [P, SEQ]) for n in ("k_cos", "k_sin", "q_cos", "q_sin"))
        qT = sb("qT", [P, 2, SEQ])
        kv_win = sb("kv_win", [P, 2, 8, 2, SEG])
        k_own = sb("k_own", [P, 2, HEADS, SEQ])
        V_STEP = 4 * P + 2 * HD
        v_own = sb("v_own", [P, 2, 2 * V_STEP])
        row_max = sb("row_max", [P, 2, 32])
        neg_max, rest1 = sb("neg_max", [32, 64]), sb("rest1", [32, 64])
        part2 = sb("part2", [32, 64], BF16)
        max_part = sb("max_part", [96, 2, P], BF16)
        prob = sb("prob", [P, 2, 1024])
        prob_t = sb("prob_t", [P, 2, 1024])
        tree = sb("tree", [P, 32, 16])
        tree2 = sb("tree2", [P, 32, 8])
        tree3 = sb("tree3", [P, 32, 4])
        tree4 = sb("tree4", [P, 32, 2])
        key_sum = sb("key_sum", [P, 32])
        inverse = sb("inverse", [32, 64])
        inverse_sb = sb("inverse_sb", [P, 2, P])
        headed = sb("headed", [P, 2, 2, P])
        resid = sb("resid", [P, 2, P])
        stats, mean_var, veps, rstd = sb("stats", [P, 6]), sb("mean_var", [P, 2, 2]), sb("veps", [P, 1]), sb("rstd", [P, 2, 1])
        mean_neg = sb("mean_neg", [P, 2, 1])
        mean_part = sb("mean_part", [P, 2, 1])
        row = sb("row", [P, 4, ROW])
        x1T = sb("x1T", [P, 2, P])
        score, at_top, keyed = (sb(n, [P, 2, 8]) for n in ("score", "at_top", "keyed"))
        top, ktop = sb("top", [P, 2]), sb("ktop", [P, 2])
        chosen = sb("chosen", [P, 2, 8], BF16)
        base = sb("base", [P, 2, 8])
        place8, place_prod, place = sb("place8", [P, 2, 8]), sb("place_prod", [P, 2, 8]), sb("place", [P, 2])
        place_i = sb("place_i", [P, 4], I32)

        pad = sb("pad", [P, ROW])
        pad_at, pad_i = sb("pad_at", [P, 8]), sb("pad_i", [P, 8], I32)
        count8 = sb("count8", [1, 8])
        over, tiles8 = sb("over", [1, 8, 64]), sb("tiles8", [1, 8])
        cum_prod, cum8, jump8 = sb("cum_prod", [1, 8, 8]), sb("cum8", [1, 8]), sb("jump8", [1, 8])
        past, past_jump = sb("past", [1, TILES, 8]), sb("past_jump", [1, TILES, 8])
        tile_e, tile_j, tile_row = sb("tile_e", [1, TILES]), sb("tile_j", [1, TILES]), sb("tile_row", [1, TILES])
        tile_e_i, tile_row_i = sb("tile_e_i", [1, TILES], I32), sb("tile_row_i", [1, TILES], I32)

        rows_in = sb("rows_in", [P, RING, ROW])
        rowsT = sb("rowsT", [P, 2, P])
        hid = sb("hid", [P, 2, FF])
        hidT = sb("hidT", [P, 2, FF])
        sum2 = sb("sum2", [P, 2, P])
        stats2, mv2 = sb("stats2", [P, 6]), sb("mv2", [P, 2, 2])
        veps2, rstd2 = sb("veps2", [P, 1]), sb("rstd2", [P, 2, 1])
        done_rows = sb("done_rows", [P, RING, P])
        token_i = sb("token_i", [P, RING], I32)

        S = psum("S", [P, 4, 512])
        O = psum("O", [P, 2, 512])
        B6 = psum("B6", [P, 512])
        B7 = psum("B7", [P, 512])

        weights_in, experts_in, biases_in, bias_parts_in = sem("weights_in"), sem("experts_in"), sem("biases_in"), sem("bias_parts_in")
        x_loaded = [sem(f"x_loaded{i}") for i in range(2)]
        setup_dve, setup_pool = sem("setup_dve"), sem("setup_pool")
        xT_made, xT_ready = sem("xT_made"), sem("xT_ready")
        k_made, k_turned, k_ready = sem("k_made"), sem("k_turned"), sem("k_ready")
        k_own_ready = [sem(f"k_own_ready{i}") for i in range(2)]
        q_made, q_turned, q_ready = sem("q_made"), sem("q_turned"), sem("q_ready")
        v_made, v_ready = sem("v_made"), sem("v_ready")
        x_bias_ready = sem("x_bias_ready")
        k_own_zero, rot_made, projection_read = (sem(n) for n in ("k_own_zero", "rot_made", "projection_read"))
        scores_made, max_ready, max_turned = sem("scores_made"), sem("max_ready"), sem("max_turned")
        neg_ready, part1_ready, part2_ready, max_parts_ready = (
            sem(n) for n in ("neg_ready", "part1_ready", "part2_ready", "max_parts_ready"))
        shifted, prob_ready, prob_t_ready = sem("shifted"), sem("prob_ready"), sem("prob_t_ready")
        tree_step, key_sum_ready, total_made, inverse_ready, inverse_wide, inverse_copied = (
            sem(n) for n in ("tree_step", "key_sum_ready", "total_made", "inverse_ready", "inverse_wide", "inverse_copied"))
        values_made, headed_ready = sem("values_made"), sem("headed_ready")
        attn_made, resid_ready, stats_ready, mv_ready, veps_ready, inv_ready, rstd_ready = (
            sem(n) for n in ("attn_made", "resid_ready", "stats_ready", "mv_ready", "veps_ready", "inv_ready", "rstd_ready"))
        row_ready, x1T_made, x1T_ready, route_made = sem("row_ready"), sem("x1T_made"), sem("x1T_ready"), sem("route_made")
        score_ready, top_ready, at_top_ready, keyed_ready, ktop_ready, chosen_ready = (
            sem(n) for n in ("score_ready", "top_ready", "at_top_ready", "keyed_ready", "ktop_ready", "chosen_ready"))
        rank_made, place8_ready, place_prod_ready, place_ready, place_i_ready, base_ready = (
            sem(n) for n in ("rank_made", "place8_ready", "place_prod_ready", "place_ready", "place_i_ready", "base_ready"))
        token_set = sem("token_set")
        row_out = [sem(f"row_out{i}") for i in range(4)]
        table_step, table_ready, pad_at_ready, pads_out = sem("table_step"), sem("table_ready"), sem("pad_at_ready"), sem("pads_out")
        pads_out_sp = sem("pads_out_sp")
        rows_loaded = [sem(f"rows_loaded{i}") for i in range(RING)]
        rowsT_made, rowsT_ready, hid_made, hid_ready, hidT_made, hidT_ready, y_made = (
            sem(n) for n in ("rowsT_made", "rowsT_ready", "hid_made", "hid_ready", "hidT_made", "hidT_ready", "y_made"))
        sum2_ready, stats2_ready, mv2_ready, veps2_ready, rstd2_ready, done_ready, token_ready = (
            sem(n) for n in ("sum2_ready", "stats2_ready", "mv2_ready", "veps2_ready", "rstd2_ready", "done_ready", "token_ready"))
        tile_out = [sem(f"tile_out{i}") for i in range(RING)]

        WEIGHTS = 16 * 11

        def held(eng, count):
            return count if isinstance(count, int) else eng.compute_val(count)

        def settled(eng):
            eng.wait_ge(setup_pool, 1)

        def unit_loop(eng, slot):
            for k in range(12):
                slot(k, k // 4 * 2, k, k, k % 4)
            with eng.Fori(0, (UNITS - 16) // 8) as r:
                for half in range(2):
                    k0, b0 = eng.snap(r * 8 + (12 + 4 * half)), eng.snap(r * 4 + (6 + 2 * half))
                    for j in range(4):
                        slot(k0 + j, b0, 12, UNITS - 5, j)
            for j in range(4):
                k = UNITS - 4 + j
                slot(k, UNITS // 2 - 2, k, k, j)

        def tile_loop(eng, slot):
            for t in range(2 * RING):
                slot(t, t // RING, t, t, t % RING)
            with eng.Fori(2, TILES // RING - 1) as r:
                t0 = eng.snap(r * RING)
                for j in range(RING):
                    slot(t0 + j, r, 2 * RING, TILES - RING - 1, j)
            for j in range(RING):
                t = TILES - RING + j
                slot(t, TILES // RING - 1, t, t, j)

        block = ctx.enter_context(nc.Block())

        @block.sync
        def _(sp):
            sp.dma_start(cf_sb[:, :], cf).then_inc(weights_in, 16)
            sp.dma_start(x_in[:, 0], x_rows[0]).then_inc(x_loaded[0], 16)
            sp.dma_start(wq_sb[:, :], wq).then_inc(weights_in, 16)
            sp.dma_start(wkv_sb[:, :], wkv).then_inc(weights_in, 16)
            sp.dma_start(x_in[:, 1], x_rows[1]).then_inc(x_loaded[1], 16)
            sp.dma_start(cb_sb[:, :], cb).then_inc(weights_in, 16)
            sp.dma_start(wo_sb[:, :], wo).then_inc(weights_in, 16)
            sp.dma_start(wo0_sb[:, :], wo0).then_inc(weights_in, 16)
            sp.dma_start(wr_sb[:, :], wr).then_inc(weights_in, 16)
            sp.dma_start(br_sb[:, :], br.partition_broadcast(P)).then_inc(weights_in, 16)
            sp.dma_start(bo_sb[:, 1], bo.partition_broadcast(P)).then_inc(weights_in, 16)
            sp.dma_start(bo_sb[SEG:P, 0], bo.partition_broadcast(P - SEG)).then_inc(weights_in, 16)
            sp.dma_start(bo_sb[0:SEG, 0], bo0.partition_broadcast(SEG)).then_inc(weights_in, 16)
            sp.dma_start(bias_in[:, 0:FF], b1).then_inc(biases_in, 16)
            sp.dma_start(bias_in[:, FF:], b2).then_inc(biases_in, 16)
            sp.dma_start(w1_sb[:, :].rearrange("p (e f) -> p e f", e=EXPERTS), w1.rearrange("e h f -> h e f")).then_inc(experts_in, 16)
            sp.dma_start(w2_sb[:, :].rearrange("p (e c n) -> p e c n", e=EXPERTS, c=CH),
                         w2.rearrange("e (c p) n -> p e c n", p=P)).then_inc(experts_in, 16)
            def load(batch, par):
                sp.wait_ge(x_bias_ready, batch - 1)
                sp.wait_ge(xT_made, batch - 1)
                sp.dma_start(x_in[:, par], x_rows[bass.ds(batch, 1)].rearrange("b p c d -> (b p) c d")
                             if not isinstance(batch, int) else x_rows[batch]).then_inc(x_loaded[par], 16)

            def spread_k(batch, par):
                sp.wait_ge(k_ready, batch + 1)
                for h in range(HEADS):
                    rows = slice(HD * h, HD * h + HD)
                    sp.dma_start(k_own[rows, par, h].rearrange("p (s k) -> p s k", k=SEG), kv_win[rows, par, :, 1]).then_inc(k_own_ready[par], 16)

            sp.wait_ge(k_own_zero, 1)
            with sp.Fori(1, BATCHES // 2) as r:
                b0 = sp.snap(r * 2)
                for par in range(2):
                    load(b0 + par, par)
                    spread_k(b0 + (par - 1), 1 - par)
            spread_k(BATCHES - 1, 1)
            sp.wait_ge(setup_dve, 7)
            for part in range(3):
                sp.dma_start(bias3[part:part + 1].rearrange("a e n -> a (e n)"),
                             bias_part[:, part, :]).then_inc(bias_parts_in, 16)

            sp.wait_ge(setup_pool, 5)
            sp.wait_ge(pad_at_ready, 1)
            for e in range(EXPERTS // 2, EXPERTS):
                at = sp.value_load(pad_i[0:1, e:e + 1], min_val=0, max_val=EXPERTS * REGION)
                sp.dma_start(routed[bass.ds(at, P), :], pad[:, :]).then_inc(pads_out_sp, 16)

            sp.wait_ge(table_ready, 1)
            for i in range(4):
                sp.wait_ge(row_out[i], 16 * (UNITS // 4))
            sp.wait_ge(pads_out, 16 * (EXPERTS // 2 + 1))
            sp.wait_ge(pads_out_sp, 16 * (EXPERTS // 2))

            def slot(t, r, lo, hi, j):
                if lo >= RING:
                    sp.wait_ge(sum2_ready, t - (RING - 1))
                    sp.wait_ge(token_ready, t - (RING - 1))
                at = sp.value_load(tile_row_i[0:1, bass.ds(t, 1)], min_val=0, max_val=EXPERTS * REGION)
                sp.dma_start(rows_in[:, j], routed[bass.ds(at, P), :]).then_inc(rows_loaded[j], 16)

            tile_loop(sp, slot)
            for i in range(RING):
                sp.wait_ge(tile_out[i], 16 * (TILES // RING))

        @block.tensor
        def _(pe):
            def turn_x(batch, par):
                pe.wait_ge(x_loaded[par], (batch // 2 + 1) * 16 if isinstance(batch, int) else batch * 8 + (8 if par else 16))
                for c in range(2):
                    mm = pe.transpose(B6[:, c * P:(c + 1) * P], x_in[:, par, c], ident)
                mm.then_inc(xT_made, 1)

            def project(batch, par, w, made):
                pe.wait_ge(xT_ready, batch + 1)
                pe.matmul(B6[:, 0:SEQ], w[:, :], xT[:, par], start=True, stop=True).then_inc(made, 1)

            def turn_v(batch, par):
                pe.wait_ge(k_ready, batch + 1)
                for pair in range(4):
                    mm = pe.transpose(B6[:, pair * P:(pair + 1) * P],
                                      kv_win[:, par, 2 * pair:2 * pair + 2].rearrange("p s b k -> p (s b k)"), ident)
                mm.then_inc(v_made, 1)

            def masks(c):
                for pair in range(2):
                    pe.matmul(S[:, 2 * c + pair], ident_b, mask[:, min(c + pair, 1)], start=True, stop=False, skip_group_check=True)

            def scores(c, par, pair):
                for s2 in range(2):
                    for blk in range(2):
                        s = 4 * c + 2 * pair + s2
                        if s - 1 + blk < 0:
                            continue
                        quad = 32 * (2 * s2 + blk)
                        mm = pe.matmul(S[quad:quad + 32, 2 * c + pair], qT[:, par, SEG * s:SEG * s + SEG],
                                       k_own[:, par, :, SEG * (s - 1 + blk):SEG * (s + blk)],
                                       start=False, stop=False, skip_group_check=True)
                if pair == 1:
                    mm.then_inc(scores_made, 1)

            def shift(c, ring):
                for pair in range(2):
                    mm = pe.matmul(S[:, 2 * c + pair], max_part[:, ring], pick[:, pair], start=False, stop=True,
                                   skip_group_check=True)
                mm.then_inc(shifted, 1)

            def slot(k, b, lo, hi, j):
                c, par = j % 2, j // 2
                nv, nx, nq = b + j // 2 + 1, b + j // 2 + 2, b + (j + 3) // 2
                prep_v = j % 2 == 0 and hi // 2 + 1 < BATCHES
                prep_x = j % 2 == 0 and hi // 2 + 2 < BATCHES
                prep_q = j % 2 == 1 and (hi + 3) // 2 < BATCHES
                pe.wait_ge(max_parts_ready, k + 1)
                shift(c, c)
                if lo >= 1:
                    if lo >= 5 and j % 2:
                        pe.wait_ge(base_ready, b + (j - 1) // 2 - 1)
                    spread_inverse(k - 1)
                if prep_v and lo >= 4:
                    pe.wait_ge(x1T_ready, b + j // 2 - 1)
                if prep_v:
                    turn_v(nv, (j // 2 + 1) % 2)
                if prep_q:
                    pe.wait_ge(neg_ready, k + 1)
                    project(nq, (j + 3) // 2 % 2, wq_sb, q_made)
                if hi + 1 < UNITS:
                    if j % 2 == 1:
                        batches, spread = held(pe, b + (j + 1) // 2 + 1), held(pe, b * (8 * HEADS) + ((j + 1) // 4 + 1) * (16 * HEADS))
                        settled(pe)
                        pe.wait_ge(q_ready, batches)
                        pe.wait_ge(k_own_ready[(j + 1) // 2 % 2], spread)
                    scores((c + 1) % 2, (j + 1) // 2 % 2, 0)
                if lo >= 4 and j % 2 == 0:
                    pe.wait_ge(inverse_copied, k)
                    route(b + j // 2 - 2)
                if prep_x:
                    pe.wait_ge(v_ready, nv + 1)
                    turn_x(nx, j // 2 % 2)
                if hi + 1 < UNITS:
                    scores((c + 1) % 2, (j + 1) // 2 % 2, 1)
                if lo >= 1:
                    output(k - 1, (c + 1) % 2, b + j // 2 - 1 if lo >= 4 and j % 2 == 0 else None)
                if prep_x:
                    project(nx, j // 2 % 2, wkv_sb, k_made)
                if hi + 2 < UNITS:
                    pe.wait_ge(prob_ready, k + 1)
                    masks(c)
                if hi + 1 < UNITS:
                    if prep_x or prep_q:
                        pe.wait_ge(projection_read, k + 5)
                    elif prep_v:
                        pe.wait_ge(v_ready, nv + 1)
                    if lo >= 3 and j % 2:
                        turn_rows_of_pair(b + (j + 1) // 2 - 2, (j + 1) % 4)
                    turn_maxima(k + 1, (c + 1) % 2)
                values(k, b, lo, j)
                if lo >= 1:
                    pe.wait_ge(resid_ready, k)
                if lo >= 4 and j % 2 == 0:
                    rank(b + j // 2 - 2)
                totals(k)
                if hi + 2 < UNITS:
                    masks(c)

            def turn_maxima(u, c):
                pe.wait_ge(max_ready, u + 1)
                pe.transpose(B6[0:32, 0:P], row_max[:, c], ident).then_inc(max_turned, 1)

            def turn_rows_of_pair(m, ring):
                pe.wait_ge(row_ready, 2 * m + 2)
                for i in range(2):
                    mm = pe.transpose(B6[:, P * (i + 1):P * (i + 2)], row[:, ring + i, 0:P], ident)
                mm.then_inc(x1T_made, 1)

            def route(m):
                pe.wait_ge(x1T_ready, m + 1)
                for i in range(2):
                    mm = pe.matmul(B7[:, P + 8 * i:P + 8 * i + 8], x1T[:, i], wr_sb[:, :], start=True, stop=True)
                mm.then_inc(route_made, 1)

            def totals(u):
                pe.wait_ge(key_sum_ready, u + 1)
                pe.matmul(B7[0:32, P:P + WIN], key_sum[:, :], cfs("pairs"), start=True, stop=True).then_inc(total_made, 1)

            def spread_inverse(u):
                pe.wait_ge(inverse_ready, u + 1)
                for pair in range(2):
                    mm = pe.matmul(B7[:, 64 * pair:64 * pair + 64], cfs("heads", 32)[:, pair * P:(pair + 1) * P], inverse[:, :],
                                   start=True, stop=True)
                mm.then_inc(inverse_wide, 1)

            def values(k, b, lo, j):
                c, par = j % 2, j // 2
                probs, batches = held(pe, k + 1), held(pe, b + j // 2 + 1)
                settled(pe)
                pe.wait_ge(prob_t_ready, probs)
                if lo >= 1:
                    pe.wait_ge(headed_ready, k)
                if j % 2 == 0:
                    pe.wait_ge(v_ready, batches)
                for s2 in range(2):
                    rows = slice(64 * s2, 64 * s2 + 64)
                    for pair in range(2):
                        for a in range(2):
                            for g in range(4):
                                v_at = (V_STEP - 2 * HD) * a + P * (2 * c + pair) + 32 * g
                                p_at = 512 * pair + 128 * g + 64 * a
                                mm = pe.matmul(O[32 * g:32 * g + 32, s2, 0:P].rearrange("p (h r i) -> p h r i", h=2, r=2)[:, :, pair],
                                               v_own[rows, par, v_at:v_at + 32], prob_t[rows, c, p_at:p_at + 64],
                                               start=(a == 0), stop=(a == 1))
                mm.then_inc(values_made, 1)

            def output(u, c, scored):
                pe.wait_ge(headed_ready, u + 1)
                pe.wait_ge(inverse_copied, u + 1)
                if scored is not None:
                    pe.wait_ge(score_ready, scored)
                for h in range(2):
                    mm = pe.matmul(B7[:, 0:P], headed[:, c, h], wo_own[:, h], start=(h == 0), stop=(h == 1))
                if c == 0:
                    for h in range(2):
                        mm = pe.matmul(B7[0:SEG, 0:P], headed[:, c, h, 0:SEG], wo0_own[:, h], start=(h == 0), stop=(h == 1))
                mm.then_inc(attn_made, 1)

            def rank(m):
                pe.wait_ge(chosen_ready, m + 1)
                both = chosen[:, :, :].rearrange("p a e -> p (a e)")
                pe.matmul(B7[:, 0:16], cbs("below"), both, start=True, stop=False, skip_group_check=True)
                pe.matmul(B7[:, 8:16], cbs("ones"), chosen[:, 0], start=False, stop=True, skip_group_check=True)
                pe.matmul(B7[:, 16:24], cbs("ones"), chosen[:, 0], start=True, stop=False, skip_group_check=True)
                pe.matmul(B7[:, 16:24], cbs("ones"), chosen[:, 1], start=False, stop=True, skip_group_check=True).then_inc(rank_made, 1)

            pe.wait_ge(weights_in, WEIGHTS)
            pe.wait_ge(setup_dve, 1)
            turn_x(0, 0)
            project(0, 0, wkv_sb, k_made)
            pe.wait_ge(k_turned, 1)
            turn_x(1, 1)
            pe.wait_ge(xT_ready, 2)
            project(0, 0, wq_sb, q_made)
            masks(0)
            masks(1)
            pe.wait_ge(q_turned, 1)
            turn_v(0, 0)
            pe.wait_ge(v_ready, 1)
            project(1, 1, wkv_sb, k_made)
            pe.wait_ge(k_own_ready[0], 16 * HEADS)
            pe.wait_ge(q_ready, 1)
            scores(0, 0, 0)
            scores(0, 0, 1)
            pe.wait_ge(k_turned, 2)
            project(1, 1, wq_sb, q_made)
            pe.wait_ge(q_turned, 2)
            turn_maxima(0, 0)
            unit_loop(pe, slot)

            last = UNITS - 1
            pe.wait_ge(base_ready, UNITS // 2 - 2)
            spread_inverse(last)
            pe.wait_ge(inverse_copied, UNITS)
            output(last, 1, None)
            for m in (UNITS // 2 - 2, UNITS // 2 - 1):
                turn_rows_of_pair(m, m % 2 * 2)
                if m == UNITS // 2 - 2:
                    pe.wait_ge(resid_ready, UNITS)
                else:
                    pe.wait_ge(base_ready, m)
                route(m)
                rank(m)

            ones3 = cbs("ones", 3)

            def turn_rows(t, r, tlo, j):
                pe.wait_ge(rows_loaded[j], r * 16 + 16)
                if tlo >= 2:
                    pe.wait_ge(rowsT_ready, t)
                pe.transpose(B6[:, 0:P], rows_in[:, j, 0:P], ident).then_inc(rowsT_made, 1)

            def first_product(t, tlo, j):
                e = pe.value_load(tile_e_i[0:1, bass.ds(t, 1)], min_val=0, max_val=EXPERTS - 1)
                pe.wait_ge(rowsT_ready, t + 1)
                if tlo >= 2:
                    pe.wait_ge(hid_ready, t - 1)
                pe.matmul(S[:, j % 2], ones3, b13[:, bass.ds(e * (FF + P), FF)], start=True, stop=False)
                pe.matmul(S[:, j % 2], rowsT[:, j % 2], w1_sb[:, bass.ds(e * FF, FF)], start=False, stop=True).then_inc(hid_made, 1)

            def turn_hidden(t, tlo, j):
                pe.wait_ge(hid_ready, t + 1)
                if tlo >= 2:
                    pe.wait_ge(hidT_ready, t - 1)
                for c in range(CH):
                    mm = pe.transpose(S[:, 2 + j % 2, c * P:(c + 1) * P], hid[:, j % 2, c * P:(c + 1) * P], ident)
                mm.then_inc(hidT_made, 1)

            def second_product(t, tlo, j):
                e = pe.value_load(tile_e_i[0:1, bass.ds(t, 1)], min_val=0, max_val=EXPERTS - 1)
                pe.wait_ge(hidT_ready, t + 1)
                if tlo >= 2:
                    pe.wait_ge(sum2_ready, t - 1)
                for c in range(CH):
                    pe.matmul(O[:, j % 2, 0:P], hidT[:, j % 2, c * P:(c + 1) * P],
                              w2_sb[:, bass.ds(e * (CH * P) + c * P, P)], start=(c == 0), stop=False)
                pe.matmul(O[:, j % 2, 0:P], ones3, b13[:, bass.ds(e * (FF + P) + FF, P)], start=False,
                          stop=True).then_inc(y_made, 1)

            b13 = bias3[:, :, :].rearrange("a e n -> a (e n)")
            pe.wait_ge(table_ready, 1)
            pe.wait_ge(bias_parts_in, 48)
            pe.wait_ge(experts_in, 32)
            turn_rows(0, 0, 0, 0)
            pe.wait_ge(rowsT_ready, 1)
            turn_rows(1, 0, 1, 1)
            first_product(0, 0, 0)

            def tile_slot(t, r, lo, hi, j):
                if hi + 2 < TILES:
                    turn_rows(t + 2, r + (j + 2) // RING, lo + 2, (j + 2) % RING)
                if hi + 1 < TILES:
                    first_product(t + 1, lo + 1, (j + 1) % RING)
                if lo >= 1:
                    second_product(t - 1, lo - 1, (j - 1) % RING)
                turn_hidden(t, lo, j)

            tile_loop(pe, tile_slot)
            second_product(TILES - 1, TILES - 1, RING - 1)

        @block.vector
        def _(dve):
            dve.memset(k_own[:, 1].rearrange("p h n -> p (h n)"), 0.0).then_inc(k_own_zero, 1)
            dve.wait_ge(weights_in, WEIGHTS)
            for h in range(2):
                dve.tensor_scalar(wo_own[:, h], wo_sb[:, :], cfs("own2")[:, h:h + 1], None, ALU.mult)
                dve.tensor_scalar(wo0_own[:, h], wo0_sb[:, :], cfs("own2")[:, h:h + 1], None, ALU.mult)
            dve.tensor_copy(base[:, 1], cfs("first")).then_inc(setup_dve, 1)
            dve.memset(max_part[:, :, :], 0.0).then_inc(setup_dve, 1)
            def turn(batch, made, free, by_cos, by_sin, blo):
                dve.wait_ge(made, batch + 1)
                if blo >= 1:
                    dve.wait_ge(free, batch)
                dve.tensor_tensor(by_sin[:, :], B6[:, 0:SEQ], cfs("sin"), ALU.mult).then_inc(rot_made, 1)
                dve.tensor_tensor(by_cos[:, :], B6[:, 0:SEQ], cfs("cos"), ALU.mult).then_inc(projection_read, 1)

            def swap_halves(by_sin, turned, turns):
                turns = held(dve, turns)
                settled(dve)
                dve.wait_ge(rot_made, turns)
                dve.stream_shuffle(by_sin[:, :], by_sin[:, :], [i ^ (HD // 2) for i in range(32)]).then_inc(turned, 1)

            def row_maximum(u, c):
                dve.wait_ge(scores_made, u + 1)
                dve.tensor_reduce(row_max[:, c], S[:, 2 * c:2 * c + 2].rearrange("p a (g k) -> p (a g) k", k=SEG),
                                  AX.X, ALU.max).then_inc(max_ready, 1)

            def max_parts(k, c):
                dst = max_part[:, c].rearrange("m (s b i) -> m s b i", s=2, b=2)

                def by_segment(a):
                    return a[:, :].rearrange("m (s i) -> m s i", s=2)

                def wide(a):
                    return by_segment(a).unsqueeze(2).to_broadcast([32, 2, 2, SEG])

                dve.wait_ge(max_turned, k + 1)
                dve.tensor_reduce(by_segment(neg_max), B6[0:32, 0:P].rearrange("m (s b i) -> m s i b", s=2, b=2),
                                  AX.X, ALU.max, negate=True).then_inc(neg_ready, 1)
                if not isinstance(k, int) or k >= 2:
                    deviation(k - 2, c)
                dve.wait_ge(neg_ready, k + 1)
                dve.tensor_copy(dst[0:32], wide(neg_max)).then_inc(part1_ready, 1)
                dve.wait_ge(part1_ready, k + 1)
                dve.tensor_tensor(by_segment(rest1), by_segment(neg_max), dst[0:32, :, 0], ALU.subtract)
                dve.tensor_tensor(by_segment(part2), by_segment(neg_max), dst[0:32, :, 0], ALU.subtract).then_inc(part2_ready, 1)
                dve.tensor_tensor(dst[32:64], wide(neg_max), dst[0:32], ALU.subtract)
                dve.wait_ge(part2_ready, k + 1)
                dve.tensor_tensor(dst[64:96], wide(rest1), wide(part2), ALU.subtract).then_inc(max_parts_ready, 1)

            def invert(u):
                dve.wait_ge(total_made, u + 1)
                dve.reciprocal(inverse[:, :], B7[0:32, P:P + WIN]).then_inc(inverse_ready, 1)

            def divide(u, c):
                dve.wait_ge(inverse_copied, u + 1)
                dve.wait_ge(values_made, u + 1)
                dve.tensor_tensor(headed[:, c].rearrange("p h (r s i) -> p s (h r) i", r=2, s=2),
                                  O[:, :, 0:P].rearrange("p s (q i) -> p s q i", i=SEG),
                                  inverse_sb[:, :, :].rearrange("p h (r s i) -> p s (h r) i", r=2, s=2),
                                  ALU.mult).then_inc(headed_ready, 1)

            def both(a):
                return a.unsqueeze(1).to_broadcast([P, 2, 8])

            def all8(a):
                return a[:, :].unsqueeze(2).to_broadcast([P, 2, 8])

            def add_score(m):
                dve.wait_ge(route_made, m + 1)
                dve.tensor_tensor(score[:, :, :], B7[:, P:P + 16].rearrange("p (a e) -> p a e", a=2), both(br_sb[:, :]),
                                  ALU.add).then_inc(score_ready, 1)

            def top_score(m):
                dve.wait_ge(score_ready, m + 1)
                dve.tensor_reduce(top[:, :], score[:, :, :], AX.X, ALU.max).then_inc(top_ready, 1)

            def find_top(m):
                dve.wait_ge(top_ready, m + 1)
                dve.tensor_tensor(at_top[:, :, :], score[:, :, :], all8(top), ALU.is_ge).then_inc(at_top_ready, 1)

            def key_experts(m):
                dve.wait_ge(at_top_ready, m + 1)
                dve.tensor_tensor(keyed[:, :, :], at_top[:, :, :], both(cfs("rev")), ALU.mult).then_inc(keyed_ready, 1)

            def top_key(m):
                dve.wait_ge(keyed_ready, m + 1)
                dve.tensor_reduce(ktop[:, :], keyed[:, :, :], AX.X, ALU.max).then_inc(ktop_ready, 1)

            def one_hot(m):
                dve.wait_ge(ktop_ready, m + 1)
                dve.tensor_tensor(chosen[:, :, :], both(cfs("rev")), all8(ktop), ALU.is_equal).then_inc(chosen_ready, 1)

            def add_residual(u, c, ring):
                dve.wait_ge(attn_made, u + 1)
                dve.wait_ge(x_bias_ready, add_residual.batch + 1)
                dve.tensor_tensor(resid[:, c], B7[:, 0:P], x_bias[:, ring], ALU.add).then_inc(resid_ready, 1)

            def deviation_parts(u, c):
                dve.wait_ge(resid_ready, u + 1)
                dve.bn_stats(stats[:, :], resid[:, c]).then_inc(stats_ready, 1)

            def deviation(u, c):
                units = held(dve, u + 1)
                settled(dve)
                dve.wait_ge(stats_ready, units)
                dve.bn_aggr(mean_var[:, c], stats[:, :]).then_inc(mv_ready, 1)

            def add_places(m, c):
                new, old = c, (c + 1) % 2
                dve.wait_ge(rank_made, m + 1)
                if not isinstance(m, int) or m >= 1:
                    dve.wait_ge(base_ready, m)
                dve.tensor_tensor(place8[:, :, :], B7[:, 0:16].rearrange("p (a e) -> p a e", a=2), both(base[:, old]),
                                  ALU.add).then_inc(place8_ready, 1)
                dve.tensor_tensor(base[:, new], B7[:, 16:24], base[:, old], ALU.add).then_inc(base_ready, 1)

            def pick_places(m):
                dve.wait_ge(place8_ready, m + 1)
                dve.tensor_tensor(place_prod[:, :, :], place8[:, :, :], chosen[:, :, :], ALU.mult).then_inc(place_prod_ready, 1)

            def sum_places(m):
                dve.wait_ge(place_prod_ready, m + 1)
                dve.tensor_reduce(place[:, :], place_prod[:, :, :], AX.X, ALU.add).then_inc(place_ready, 1)

            def positions(m, ring):
                dve.wait_ge(place_ready, m + 1)
                if not isinstance(positions.sent, int) or positions.sent > 0:
                    for i in range(2):
                        dve.wait_ge(row_out[ring + i], positions.sent)
                dve.tensor_copy(place_i[:, ring:ring + 2], place[:, :]).then_inc(place_i_ready, 1)

            def turn_probs(u, c):
                dve.wait_ge(prob_ready, u + 1)
                dve.transpose(prob_t[:, c], prob[:, c]).then_inc(prob_t_ready, 1)

            def slot(k, b, lo, hi, j):
                c = j % 2
                o = (c + 1) % 2
                nv, nx, nq = b + j // 2 + 1, b + j // 2 + 2, b + (j + 3) // 2
                prep_v = j % 2 == 0 and hi // 2 + 1 < BATCHES
                prep_x = j % 2 == 0 and hi // 2 + 2 < BATCHES
                prep_q = j % 2 == 1 and (hi + 3) // 2 < BATCHES
                m = b + j // 2 - 2 if lo >= 4 and j % 2 == 0 else None
                placed = b + j // 2 - 2 if lo >= 5 and j % 2 else None
                if placed is not None:
                    positions.sent = 16 * (placed // 2) if isinstance(k, int) else b * 8 - 16
                max_parts(k, c)
                if lo >= 1:
                    invert(k - 1)
                if placed is not None:
                    add_places(placed, j // 2)
                    pick_places(placed)
                    sum_places(placed)
                turn_probs(k, c)
                if lo >= 1:
                    divide(k - 1, o)
                if m is not None:
                    add_score(m)
                if placed is not None:
                    positions(placed, j - 1)
                if hi + 1 < UNITS:
                    row_maximum(k + 1, o)
                if m is not None:
                    top_score(m)
                if prep_x:
                    turn(nx, k_made, k_ready, k_cos, k_sin, 2)
                if prep_q:
                    turn(nq, q_made, q_ready, q_cos, q_sin, 2)
                if m is not None:
                    find_top(m)
                if lo >= 1:
                    add_residual.batch = b + (j - 1) // 2
                    add_residual(k - 1, o, (j - 1) % 4)
                if m is not None:
                    key_experts(m)
                if prep_x:
                    swap_halves(k_sin, k_turned, k + 5)
                if prep_q:
                    swap_halves(q_sin, q_turned, k + 5)
                if m is not None:
                    top_key(m)
                if lo >= 1:
                    deviation_parts(k - 1, o)
                if m is not None:
                    one_hot(m)

            turn(0, k_made, k_ready, k_cos, k_sin, 0)
            swap_halves(k_sin, k_turned, 1)
            turn(0, q_made, q_ready, q_cos, q_sin, 0)
            swap_halves(q_sin, q_turned, 2)
            dve.wait_ge(k_ready, 1)
            for h in range(HEADS):
                ins = dve.tensor_scalar(k_own[:, 0, h].rearrange("p (s k) -> p s k", k=SEG), kv_win[:, 0, :, 1],
                                        cfs("own16")[:, h:h + 1], None, ALU.mult)
            ins.then_inc(k_own_ready[0], 16 * HEADS)
            turn(1, k_made, k_ready, k_cos, k_sin, 1)
            swap_halves(k_sin, k_turned, 3)
            row_maximum(0, 0)
            turn(1, q_made, q_ready, q_cos, q_sin, 1)
            swap_halves(q_sin, q_turned, 4)
            unit_loop(dve, slot)
            last = UNITS - 1

            def choose_and_place(m):
                for step in (add_score, top_score, find_top, key_experts, top_key, one_hot):
                    step(m)
                add_places(m, m % 2)
                pick_places(m)
                sum_places(m)
                positions.sent = 16 * (m // 2)
                positions(m, m % 2 * 2)

            deviation(last - 1, 0)
            invert(last)
            divide(last, 1)
            add_residual.batch = BATCHES - 1
            add_residual(last, 1, 3)
            deviation_parts(last, 1)
            deviation(last, 1)
            dve.wait_ge(biases_in, 32)
            dve.tensor_copy(bias_part[:, 0], bias_in[:, :]).then_inc(setup_dve, 1)
            dve.wait_ge(setup_dve, 3)
            dve.tensor_tensor(bias_rest[:, 0], bias_in[:, :], bias_part[:, 0], ALU.subtract).then_inc(setup_dve, 1)
            dve.wait_ge(setup_dve, 4)
            dve.tensor_copy(bias_part[:, 1], bias_rest[:, 0]).then_inc(setup_dve, 1)
            dve.wait_ge(setup_dve, 5)
            dve.tensor_tensor(bias_rest[:, 1], bias_rest[:, 0], bias_part[:, 1], ALU.subtract).then_inc(setup_dve, 1)
            dve.wait_ge(setup_dve, 6)
            dve.tensor_copy(bias_part[:, 2], bias_rest[:, 1]).then_inc(setup_dve, 1)
            choose_and_place(UNITS // 2 - 2)
            choose_and_place(UNITS // 2 - 1)

            dve.wait_ge(base_ready, UNITS // 2)
            fill = base[:, 1]
            dve.tensor_scalar(pad_at[:, :], fill, cfs("part"), None, ALU.add).then_inc(table_step, 1)
            dve.tensor_tensor(count8[:, :], fill[0:1], cfs("first", 1), ALU.subtract).then_inc(table_step, 1)
            dve.wait_ge(table_step, 2)
            dve.tensor_copy(pad_i[:, :], pad_at[:, :]).then_inc(pad_at_ready, 1)
            dve.tensor_tensor(over[:, :, :], count8[:, :].unsqueeze(2).to_broadcast([1, 8, 64]),
                              cfs("upto", 1).unsqueeze(1).to_broadcast([1, 8, 64]), ALU.is_gt).then_inc(table_step, 1)
            dve.wait_ge(table_step, 3)
            dve.tensor_reduce(tiles8[:, :], over[:, :, :], AX.X, ALU.add).then_inc(table_step, 1)
            dve.wait_ge(table_step, 4)
            dve.tensor_tensor(cum_prod[:, :, :], tiles8[:, :].unsqueeze(1).to_broadcast([1, 8, 8]),
                              cfs("before", 1).rearrange("p (a b) -> p a b", a=8), ALU.mult).then_inc(table_step, 1)
            dve.tensor_scalar(jump8[:, :], tiles8[:, :], -float(P), float(REGION), ALU.mult, ALU.add).then_inc(table_step, 1)
            dve.wait_ge(table_step, 6)
            dve.tensor_reduce(cum8[:, :], cum_prod[:, :, :], AX.X, ALU.add).then_inc(table_step, 1)
            dve.wait_ge(table_step, 7)
            dve.tensor_tensor(past[:, :, :], cfs("tile", 1).unsqueeze(2).to_broadcast([1, TILES, 8]),
                              cum8[:, :].unsqueeze(1).to_broadcast([1, TILES, 8]), ALU.is_ge).then_inc(table_step, 1)
            dve.wait_ge(table_step, 8)
            dve.tensor_tensor(past_jump[:, :, :], past[:, :, :], jump8[:, :].unsqueeze(1).to_broadcast([1, TILES, 8]),
                              ALU.mult).then_inc(table_step, 1)
            dve.tensor_reduce(tile_e[:, :], past[:, :, :], AX.X, ALU.add).then_inc(table_step, 1)
            dve.wait_ge(table_step, 10)
            dve.tensor_reduce(tile_j[:, :], past_jump[:, :, :], AX.X, ALU.add).then_inc(table_step, 1)
            dve.tensor_scalar(tile_e_i[:, :], tile_e[:, :], float(EXPERTS - 1), None, ALU.min).then_inc(table_step, 1)
            dve.wait_ge(table_step, 12)
            dve.scalar_tensor_tensor(out=tile_row[:, :], in0=cfs("tile", 1), scalar=float(P), in1=tile_j[:, :],
                                     op0=ALU.mult, op1=ALU.add).then_inc(table_step, 1)
            dve.wait_ge(table_step, 13)
            dve.tensor_scalar(tile_row_i[:, :], tile_row[:, :], float(EXPERTS * REGION), None, ALU.min).then_inc(table_ready, 1)

            def hidden_back(t, tlo, j):
                dve.wait_ge(hidT_made, t + 1)
                dve.tensor_copy(hidT[:, j % 2], S[:, 2 + j % 2]).then_inc(hidT_ready, 1)

            def add_back(t, r, tlo, j):
                dve.wait_ge(y_made, t + 1)
                dve.tensor_tensor(sum2[:, j % 2], O[:, j % 2, 0:P], rows_in[:, j, 0:P], ALU.add).then_inc(sum2_ready, 1)
                if tlo >= RING:
                    dve.wait_ge(tile_out[j], r * 16)
                dve.tensor_copy(token_i[:, j:j + 1], rows_in[:, j, DIM:DIM + 1]).then_inc(token_ready, 1)
                dve.wait_ge(sum2_ready, t + 1)
                dve.bn_stats(stats2[:, :], sum2[:, j % 2]).then_inc(stats2_ready, 1)
                settled(dve)
                dve.wait_ge(stats2_ready, t + 1)
                dve.bn_aggr(mv2[:, j % 2], stats2[:, :]).then_inc(mv2_ready, 1)

            def normalise2(t, j):
                dve.wait_ge(rstd2_ready, t + 1)
                dve.tensor_scalar(done_rows[:, j], sum2[:, j % 2], mv2[:, j % 2, 0:1], rstd2[:, j % 2],
                                  ALU.subtract, ALU.mult).then_inc(done_ready, 1)

            def tile_slot(t, r, lo, hi, j):
                if lo >= 2:
                    normalise2(t - 2, (j - 2) % RING)
                if lo >= 1:
                    add_back(t - 1, r - (1 if j == 0 else 0), lo - 1, (j - 1) % RING)
                hidden_back(t, lo, j)

            tile_loop(dve, tile_slot)
            normalise2(TILES - 2, RING - 2)
            add_back(TILES - 1, TILES // RING - 1, TILES - 1, RING - 1)
            normalise2(TILES - 1, RING - 1)

        @block.scalar
        def _(act):
            def copy_xT(batch, par):
                act.wait_ge(xT_made, batch + 1)
                act.copy(xT[:, par], B6[:, 0:SEQ]).then_inc(xT_ready, 1)

            def copy_v(batch, par):
                act.wait_ge(v_made, batch + 1)
                act.copy(v_own[:, par].rearrange("p (a x) -> p a x", a=2)[:, :, 0:4 * P]
                         .rearrange("p a (q r) -> p a q r", r=32)[:, :, :, 0:2 * HD],
                         B6[:, :].rearrange("p (q a d) -> p a q d", a=2, d=2 * HD)).then_inc(v_ready, 1)

            def exponentials(u, c):
                act.wait_ge(shifted, u + 1)
                act.activation(prob[:, c], S[:, 2 * c:2 * c + 2].rearrange("p a n -> p (a n)"), ACT.Exp,
                               scale=SCALE).then_inc(prob_ready, 1)

            def copy_x1T(m, read):
                act.wait_ge(x1T_made, m + 1)
                if read is not None:
                    act.wait_ge(neg_ready, read)
                act.copy(x1T[:, :].rearrange("p a n -> p (a n)"), B6[:, P:3 * P]).then_inc(x1T_ready, 1)

            def normalise(u, c, ring, sent):
                act.wait_ge(rstd_ready, u + 1)
                if sent is not None:
                    act.wait_ge(row_out[ring], sent)
                act.activation(row[:, ring, 0:P], resid[:, c], ACT.Identity, bias=mean_part[:, c], scale=rstd[:, c]).then_inc(row_ready, 1)

            def copy_inverse(u):
                act.wait_ge(inverse_wide, u + 1)
                act.copy(inverse_sb[:, :, :], B7[:, 0:P].unsqueeze(1).to_broadcast([P, 2, P])).then_inc(inverse_copied, 1)

            def slot(k, b, lo, hi, j):
                c = j % 2
                nv, nx, nq = b + j // 2 + 1, b + j // 2 + 2, b + (j + 3) // 2
                prep_v = j % 2 == 0 and hi // 2 + 1 < BATCHES
                prep_x = j % 2 == 0 and hi // 2 + 2 < BATCHES
                prep_q = j % 2 == 1 and (hi + 3) // 2 < BATCHES
                if lo >= 4 and j % 2 == 0:
                    copy_x1T(b + j // 2 - 2, k + 1)
                exponentials(k, c)
                if lo >= 1:
                    copy_inverse(k - 1)
                if prep_v:
                    copy_v(nv, (j // 2 + 1) % 2)
                if prep_x:
                    copy_xT(nx, j // 2 % 2)
                if lo >= 2:
                    normalise(k - 2, c, (j + 2) % 4, None if lo < 6 else 16 * ((k - 2) // 4) if isinstance(k, int)
                              else b * 8 + (-16 if j < 2 else 0))

            copy_xT(0, 0)
            copy_xT(1, 1)
            copy_v(0, 0)
            unit_loop(act, slot)
            copy_inverse(UNITS - 1)
            normalise(UNITS - 2, 0, 2, 16 * ((UNITS - 2) // 4))
            copy_x1T(UNITS // 2 - 2, None)
            normalise(UNITS - 1, 1, 3, 16 * ((UNITS - 1) // 4))
            copy_x1T(UNITS // 2 - 1, None)

            def copy_rows(t, j):
                act.wait_ge(rowsT_made, t + 1)
                act.copy(rowsT[:, j % 2], B6[:, 0:P]).then_inc(rowsT_ready, 1)

            def gelu(t, j):
                act.wait_ge(hid_made, t + 1)
                act.activation(hid[:, j % 2], S[:, j % 2], ACT.Gelu).then_inc(hid_ready, 1)

            copy_rows(0, 0)
            copy_rows(1, 1)
            gelu(0, 0)

            def tile_slot(t, r, lo, hi, j):
                if hi + 2 < TILES:
                    copy_rows(t + 2, j)
                if hi + 1 < TILES:
                    gelu(t + 1, (j + 1) % 2)

            tile_loop(act, tile_slot)

        @block.gpsimd
        def _(pool):
            nc.gpsimd.memset(kv_win[:, :, 0, 0], 0.0).then_inc(setup_pool, 1)
            nc.gpsimd.memset(v_own[:, :, :], 0.0).then_inc(setup_pool, 1)
            nc.gpsimd.memset(row[:, :, :], 0.0).then_inc(setup_pool, 1)
            nc.gpsimd.memset(pad[:, :], 0.0).then_inc(setup_pool, 1)
            pool.wait_ge(weights_in, WEIGHTS)
            pool.wait_ge(setup_pool, 4)
            for i in range(4):
                nc.gpsimd.tensor_copy(row[:, i, DIM:DIM + 1], cfs("tok")[:, i:i + 1]).then_inc(token_set, 1)
            nc.gpsimd.tensor_scalar(pad[:, DIM:DIM + 1], cfs("part"), 1.0, float(TOKENS), ALU.mult, ALU.add).then_inc(setup_pool, 1)
            pool.wait_ge(setup_pool, 5)
            pool.dma_start(routed[EXPERTS * REGION:EXPERTS * REGION + P, :], pad[:, :]).then_inc(pads_out, 16)

            def add_k(batch, par):
                pool.wait_ge(k_turned, batch + 1)
                by_seg = [a[:, :].rearrange("p (s k) -> p s k", k=SEG) for a in (k_cos, k_sin)]
                nc.gpsimd.tensor_tensor(kv_win[:, par, :, 1], by_seg[0], by_seg[1], ALU.add)
                nc.gpsimd.tensor_tensor(kv_win[:, par, 1:, 0], by_seg[0][:, 0:7], by_seg[1][:, 0:7], ALU.add).then_inc(k_ready, 1)

            def add_q(batch, par):
                pool.wait_ge(q_turned, batch + 1)
                nc.gpsimd.tensor_tensor(qT[:, par], q_cos[:, :], q_sin[:, :], ALU.add).then_inc(q_ready, 1)

            def add_bias(batch, par, blo):
                pool.wait_ge(x_loaded[par], (batch // 2 + 1) * 16 if isinstance(batch, int) else batch * 8 + (8 if par else 16))
                if blo >= 2:
                    pool.wait_ge(resid_ready, add_bias.used)
                nc.gpsimd.tensor_tensor(x_bias[:, 2 * par:2 * par + 2], x_in[:, par], bo_sb[:, :, :], ALU.add).then_inc(x_bias_ready, 1)

            def sum_keys(u, c):
                src = prob[:, c].rearrange("p (g k) -> p g k", k=SEG)
                steps = [src, tree[:, :, :], tree2[:, :, :], tree3[:, :, :], tree4[:, :, :]]
                pool.wait_ge(prob_ready, u + 1)
                for n in range(4):
                    w = SEG >> (n + 1)
                    nc.gpsimd.tensor_tensor(steps[n + 1], steps[n][:, :, 0:w], steps[n][:, :, w:2 * w], ALU.add).then_inc(tree_step, 1)
                    pool.wait_ge(tree_step, u * 4 + n + 1)
                nc.gpsimd.tensor_tensor(key_sum[:, :].unsqueeze(2), tree4[:, :, 0:1], tree4[:, :, 1:2], ALU.add).then_inc(key_sum_ready, 1)

            def inverse_deviation(u, c):
                units = held(pool, u + 1)
                settled(pool)
                pool.wait_ge(mv_ready, units)
                nc.gpsimd.tensor_scalar(mean_neg[:, c], mean_var[:, c, 0:1], -1.0, 0.0, ALU.mult, ALU.add)
                nc.gpsimd.tensor_scalar(veps[:, :], mean_var[:, c, 1:2], 1.0, EPS, ALU.mult, ALU.add).then_inc(veps_ready, 1)
                pool.wait_ge(veps_ready, units)
                nc.gpsimd.tensor_tensor(rstd[:, c], veps[:, :], cfs("half"), ALU.pow).then_inc(inv_ready, 1)
                pool.wait_ge(inv_ready, units)
                nc.gpsimd.tensor_tensor(mean_part[:, c], mean_neg[:, c], rstd[:, c], ALU.mult).then_inc(rstd_ready, 1)

            def send(u, m, ring, ulo):
                if ulo >= 4:
                    sent = held(pool, send.sent)
                    settled(pool)
                    pool.wait_ge(row_out[ring], sent)
                    nc.gpsimd.tensor_scalar(row[:, ring, DIM:DIM + 1], row[:, ring, DIM:DIM + 1], 1.0, 4.0 * P,
                                            ALU.mult, ALU.add).then_inc(token_set, 1)
                units, pairs = held(pool, u + 1), held(pool, m + 1)
                settled(pool)
                pool.wait_ge(token_set, units if ulo >= 4 else 4)
                pool.wait_ge(place_i_ready, pairs)
                pool.wait_ge(row_ready, units)
                nc.gpsimd.indirect_dma_start(out=routed, out_offset=bass.IndirectOffsetOnAxis(ap=place_i[:, ring:ring + 1], axis=0),
                                             in_=row[:, ring], in_offset=None).then_inc(row_out[ring], 16)

            def slot(k, b, lo, hi, j):
                c = j % 2
                nv, nx, nq = b + j // 2 + 1, b + j // 2 + 2, b + (j + 3) // 2
                prep_v = j % 2 == 0 and hi // 2 + 1 < BATCHES
                prep_x = j % 2 == 0 and hi // 2 + 2 < BATCHES
                prep_q = j % 2 == 1 and (hi + 3) // 2 < BATCHES
                if j % 2 and hi + 1 < UNITS:
                    add_bias.used = k - 1
                    add_bias(b + (j + 1) // 2, (j + 1) // 2 % 2, (lo + 1) // 2)
                sum_keys(k, c)
                if lo >= 1:
                    inverse_deviation(k - 1, (c + 1) % 2)
                if prep_x:
                    add_k(nx, j // 2 % 2)
                if prep_q:
                    add_q(nq, (j + 3) // 2 % 2)
                if lo >= 5:
                    send.sent = (16 * ((k - 5) // 4) if isinstance(k, int) else b * 8 - (32 if j < 1 else 16))
                    send(k - 5, b + (j - 5) // 2, (j - 5) % 4, k - 5 if isinstance(k, int) else 4)

            add_k(0, 0)
            add_q(0, 0)
            add_bias(0, 0, 0)
            add_k(1, 1)
            add_q(1, 1)
            unit_loop(pool, slot)
            last = UNITS - 1
            inverse_deviation(last, 1)
            for u in range(last - 4, UNITS):
                send.sent = 16 * (u // 4)
                send(u, u // 2, u % 4, u)
            pool.wait_ge(pad_at_ready, 1)
            for e in range(EXPERTS // 2):
                nc.gpsimd.indirect_dma_start(out=routed, out_offset=bass.IndirectOffsetOnAxis(ap=pad_i[:, e:e + 1], axis=0),
                                             in_=pad[:, :], in_offset=None).then_inc(pads_out, 16)

            def inverse_deviation2(t, j):
                tiles = held(pool, t + 1)
                settled(pool)
                pool.wait_ge(mv2_ready, tiles)
                nc.gpsimd.tensor_scalar(veps2[:, :], mv2[:, j % 2, 1:2], 1.0, EPS, ALU.mult, ALU.add).then_inc(veps2_ready, 1)
                pool.wait_ge(veps2_ready, tiles)
                nc.gpsimd.tensor_tensor(rstd2[:, j % 2], veps2[:, :], cfs("half"), ALU.pow).then_inc(rstd2_ready, 1)

            def write_out(t, j):
                tiles = held(pool, t + 1)
                settled(pool)
                pool.wait_ge(done_ready, tiles)
                pool.wait_ge(token_ready, tiles)
                nc.gpsimd.indirect_dma_start(out=out_rows, out_offset=bass.IndirectOffsetOnAxis(ap=token_i[:, j:j + 1], axis=0),
                                             in_=done_rows[:, j], in_offset=None, bounds_check=TOKENS - 1,
                                             oob_is_err=False).then_inc(tile_out[j], 16)

            def tile_slot(t, r, lo, hi, j):
                if lo >= 1:
                    inverse_deviation2(t - 1, (j - 1) % RING)
                if lo >= 2:
                    write_out(t - 2, (j - 2) % RING)

            tile_loop(pool, tile_slot)
            inverse_deviation2(TILES - 1, RING - 1)
            write_out(TILES - 2, RING - 2)
            write_out(TILES - 1, RING - 1)


_INS = ["L0_attn_x", "L0_attn_Wq", "L0_attn_Wkv", "L0_attn_Wo", "L0_attn_bo", "L0_attn_Wo0", "L0_attn_bo0",
        "L0_ffn_wr", "L0_ffn_br", "L0_ffn_w1", "L0_ffn_b1", "L0_ffn_w2", "L0_ffn_b2"]


def kernel(**inputs):
    import concourse.bacc as bacc
    from concourse.bass_utils import run_bass_kernel_spmd as run

    nc = bacc.Bacc("TRN2", target_bir_lowering=False, num_devices=1)
    arrays, args = {}, []
    for name in _INS:
        arrays[f"in_{name}"] = np.ascontiguousarray(inputs[name])
    arrays["const_f32"], arrays["const_bf16"] = constants()
    for name, a in arrays.items():
        args.append(nc.dram_tensor(name, a.shape, mybir.dt.from_np(a.dtype), kind="ExternalInput").ap())
    args.append(nc.dram_tensor("out", (BATCHES, SEQ, DIM), F32, kind="ExternalOutput").ap())
    layer(nc, *args)
    r = run(nc, [arrays], core_ids=[0])
    return r.results[0]["out"]
```
